# Optimizing a Trainium2 kernel written in Bass

```python
import numpy as np
import jax
import jax.numpy as jnp

def _softmax(x, axis=-1):
    return jax.nn.softmax(x, axis=axis)

def _gelu(x):
    return jax.nn.gelu(x, approximate=True)

def _silu(x):
    return jax.nn.silu(x)

def _sigmoid(x):
    return jax.nn.sigmoid(x)

def _layernorm(x, axis=-1, eps=1e-05):
    m = jnp.mean(x, axis=axis, keepdims=True)
    v = jnp.var(x, axis=axis, keepdims=True)
    return (x - m) / jnp.sqrt(v + eps)

def _scatter_add(tgt, idx, src, axis=0):
    return tgt.at[idx].add(src)

def _segment_sum(src, seg, n):
    return jax.ops.segment_sum(src, seg, n)
kernel_name = 'mk_cond_resid_d4_seqx_r4_c012d0'

def setup_inputs(seed: int=0):
    np.random.seed(seed)
    _w = jnp.asarray

    def _rec_inputs():
        import jax
        import jax.numpy as jnp
        _rk = jax.random.key(seed)
        x = -0.000125 + 0.9999 * jax.random.normal(jax.random.fold_in(_rk, 1), (64, 64, 512), jnp.float32)
        _lenS = 64 - jax.random.randint(jax.random.fold_in(_rk, 7), (64,), 0, max(1, 64 // 4) + 1, jnp.int32)
        _lenS2 = 64 - jax.random.randint(jax.random.fold_in(_rk, 8), (64,), 0, max(1, 64 // 4) + 1, jnp.int32)
        itok_B_0_15 = jax.random.randint(jax.random.fold_in(_rk, 11), (64,), 0, 16, jnp.int32)
        itok_B_0_6 = jax.random.randint(jax.random.fold_in(_rk, 12), (64,), 0, 7, jnp.int32)
        itok_Bx257_0_4111 = jax.random.randint(jax.random.fold_in(_rk, 13), (64, 257), 0, 1028, jnp.int32)
        itok_B_37_3939 = jax.random.randint(jax.random.fold_in(_rk, 14), (64,), 37, 985, jnp.int32)
        itok_B_0_7 = jax.random.randint(jax.random.fold_in(_rk, 15), (64,), 0, 8, jnp.int32)
        fside_8xS_0 = -0.00162727 + 0.0609077 * jax.random.normal(jax.random.fold_in(_rk, 16), (8, 64), jnp.float32)
        return (x, itok_B_0_15, itok_B_0_6, itok_Bx257_0_4111, itok_B_37_3939, itok_B_0_7, fside_8xS_0)
    x, itok_B_0_15, itok_B_0_6, itok_Bx257_0_4111, itok_B_37_3939, itok_B_0_7, fside_8xS_0 = _rec_inputs()

    def _L0_cond_setup():
        import jax, jax.numpy as jnp
        import numpy as np
        key = jax.random.key(seed)
        k1, k2, k3, k4 = jax.random.split(key, 4)
        B, S, IN, OUT, E = (64, 64, 512, 512, 16)
        bound = 1.0 / np.sqrt(IN)
        x = jax.random.normal(k1, (B, S, IN), dtype=jnp.float32)
        idx = jax.random.randint(k2, (B,), 0, E, dtype=jnp.int64)
        W = jax.random.uniform(k3, (E, IN, OUT), dtype=jnp.float32, minval=-bound, maxval=bound)
        b = jnp.full((E, OUT), 0.1, dtype=jnp.float32)
        return {'x': x, 'id': idx, 'W': W, 'b': b}
    _L0_cond_all = _L0_cond_setup()
    _L0_cond_in = {k: v for k, v in _L0_cond_all.items() if k in ('W', 'b')}
    del _L0_cond_all

    def _L1_cond_setup():
        import jax, jax.numpy as jnp
        import numpy as np
        B, T, D_IN, D_OUT = (16, 512, 512, 512)
        N_ADAPTERS, RANK = (8, 16)
        key = jax.random.key(seed)
        k_x, k_w, k_a, k_b, k_s, k_idx = jax.random.split(key, 6)
        x = jax.random.normal(k_x, (B, T, D_IN), dtype=jnp.float32)
        W = jax.random.normal(k_w, (D_OUT, D_IN), dtype=jnp.float32) * (1.0 / np.sqrt(D_IN))
        A = jax.random.normal(k_a, (N_ADAPTERS, RANK, D_IN), dtype=jnp.float32) * 0.02
        Bm = jax.random.normal(k_b, (N_ADAPTERS, D_OUT, RANK), dtype=jnp.float32) * 0.02
        scalings = jnp.ones((N_ADAPTERS,), dtype=jnp.float32)
        adapter_idx = jax.random.randint(k_idx, (B,), 0, N_ADAPTERS, dtype=jnp.int32)
        return {'x': x, 'W': W, 'A': A, 'Bm': Bm, 'scalings': scalings, 'adapter_idx': adapter_idx}
    _L1_cond_all = _L1_cond_setup()
    _L1_cond_in = {k: v for k, v in _L1_cond_all.items() if k in ('W', 'A', 'Bm', 'scalings')}
    del _L1_cond_all

    def _L2_cond_setup():
        import jax, jax.numpy as jnp
        import numpy as np
        H, G, HD = (8, 4, 64)
        GSZ = H // G
        BLOCK = 16
        WINDOW = 256
        SCALE = 256.0 ** (-0.5)
        EPS = 1e-06
        THETA = 10000.0
        B, T, D = (16, 4, 512)
        NBLK = 257

        def _rms(x, scale):
            var = jnp.mean(x * x, axis=-1, keepdims=True)
            return x * jax.lax.rsqrt(var + EPS) * (1.0 + scale)

        def _rope(x, pos):
            half = HD // 2
            inv = 1.0 / THETA ** (jnp.arange(half, dtype=jnp.float32) / half)
            ang = pos[:, :, None].astype(jnp.float32) * inv
            cos = jnp.cos(ang)[:, None, :, :]
            sin = jnp.sin(ang)[:, None, :, :]
            x1, x2 = (x[..., :half], x[..., half:])
            return jnp.concatenate([x1 * cos - x2 * sin, x2 * cos + x1 * sin], axis=-1)
        key = jax.random.key(seed)
        ks = jax.random.split(key, 10)
        inv_d = 1.0 / np.sqrt(D)
        return {'x': jax.random.normal(ks[0], (B, T, D), jnp.float32), 'Wq': jax.random.normal(ks[1], (H * HD, D), jnp.float32) * inv_d, 'Wk': jax.random.normal(ks[2], (G * HD, D), jnp.float32) * inv_d, 'Wv': jax.random.normal(ks[3], (G * HD, D), jnp.float32) * inv_d, 'Wo': jax.random.normal(ks[4], (D, H * HD), jnp.float32) * inv_d, 'q_norm_scale': jax.random.normal(ks[5], (HD,), jnp.float32) * 0.02, 'k_norm_scale': jax.random.normal(ks[6], (HD,), jnp.float32) * 0.02, 'k_blocks': jax.random.normal(ks[7], (B * NBLK, G, BLOCK, HD), jnp.float32), 'v_blocks': jax.random.normal(ks[8], (B * NBLK, G, BLOCK, HD), jnp.float32), 'block_tables': jnp.arange(B * NBLK, dtype=jnp.int32).reshape(B, NBLK), 'kv_lens': jax.random.randint(ks[9], (B,), 0, 1024, dtype=jnp.int32)}
    _L2_cond_all = _L2_cond_setup()
    _L2_cond_in = {k: v for k, v in _L2_cond_all.items() if k in ('Wq', 'Wk', 'Wv', 'Wo', 'q_norm_scale', 'k_norm_scale', 'k_blocks', 'v_blocks')}
    del _L2_cond_all

    def _L3_cond_setup():
        import jax, jax.numpy as jnp
        import numpy as np
        B, C, T = (64, 64, 512)
        D, N = (64, 8)
        key = jax.random.key(seed)
        k_x, k_s, k_w, k_b = jax.random.split(key, 4)
        scale = 1.0 / np.sqrt(C)
        x = jax.random.normal(k_x, (B, C, T), dtype=jnp.float32)
        subjects = jax.random.randint(k_s, (B,), 0, N, dtype=jnp.int64)
        weights = jax.random.normal(k_w, (N, C, D), dtype=jnp.float32) * scale
        bias = jax.random.normal(k_b, (N, D), dtype=jnp.float32) * scale
        return {'x': x, 'subjects': subjects, 'weights': weights, 'bias': bias}
    _L3_cond_all = _L3_cond_setup()
    _L3_cond_in = {k: v for k, v in _L3_cond_all.items() if k in ('weights',)}
    del _L3_cond_all
    return {'x': x, 'itok_B_0_15': itok_B_0_15, 'itok_B_0_6': itok_B_0_6, 'itok_Bx257_0_4111': itok_Bx257_0_4111, 'itok_B_37_3939': itok_B_37_3939, 'itok_B_0_7': itok_B_0_7, 'fside_8xS_0': fside_8xS_0, 'L0_cond_W': _L0_cond_in['W'], 'L0_cond_b': _L0_cond_in['b'], 'L1_cond_W': _L1_cond_in['W'], 'L1_cond_A': _L1_cond_in['A'], 'L1_cond_Bm': _L1_cond_in['Bm'], 'L1_cond_scalings': _L1_cond_in['scalings'], 'L2_cond_Wq': _L2_cond_in['Wq'], 'L2_cond_Wk': _L2_cond_in['Wk'], 'L2_cond_Wv': _L2_cond_in['Wv'], 'L2_cond_Wo': _L2_cond_in['Wo'], 'L2_cond_q_norm_scale': _L2_cond_in['q_norm_scale'], 'L2_cond_k_norm_scale': _L2_cond_in['k_norm_scale'], 'L2_cond_k_blocks': _L2_cond_in['k_blocks'], 'L2_cond_v_blocks': _L2_cond_in['v_blocks'], 'L3_cond_weights': _L3_cond_in['weights']}

def reference(x, itok_B_0_15, itok_B_0_6, itok_Bx257_0_4111, itok_B_37_3939, itok_B_0_7, fside_8xS_0, L0_cond_W, L0_cond_b, L1_cond_W, L1_cond_A, L1_cond_Bm, L1_cond_scalings, L2_cond_Wq, L2_cond_Wk, L2_cond_Wv, L2_cond_Wo, L2_cond_q_norm_scale, L2_cond_k_norm_scale, L2_cond_k_blocks, L2_cond_v_blocks, L3_cond_weights):
    import jax
    import jax.numpy as jnp

    def _L0_cond_ref(x, id, W, b):
        import jax, jax.numpy as jnp
        import numpy as np
        Wg = W[id]
        bg = b[id]
        out = jnp.einsum('bsi,bio->bso', x, Wg) + bg[:, None, :]
        return out

    def _L1_cond_ref(x, W, A, Bm, scalings, adapter_idx):
        import jax, jax.numpy as jnp
        import numpy as np
        B, T, D_IN, D_OUT = (16, 512, 512, 512)
        N_ADAPTERS, RANK = (8, 16)
        H = jnp.einsum('btd,od->bto', x, W)
        A_b = A[adapter_idx]
        B_b = Bm[adapter_idx]
        s_b = scalings[adapter_idx]
        xa = jnp.einsum('btd,brd->btr', x, A_b)
        delta = jnp.einsum('btr,bor->bto', xa, B_b)
        delta = jax.lax.stop_gradient(delta * s_b[:, None, None])
        return H + delta

    def _L2_cond_ref(x, Wq, Wk, Wv, Wo, q_norm_scale, k_norm_scale, k_blocks, v_blocks, block_tables, kv_lens):
        import jax, jax.numpy as jnp
        import numpy as np
        H, G, HD = (8, 4, 64)
        GSZ = H // G
        BLOCK = 16
        WINDOW = 256
        SCALE = 256.0 ** (-0.5)
        EPS = 1e-06
        THETA = 10000.0
        B, T, D = (16, 4, 512)
        NBLK = 257

        def _rms(x, scale):
            var = jnp.mean(x * x, axis=-1, keepdims=True)
            return x * jax.lax.rsqrt(var + EPS) * (1.0 + scale)

        def _rope(x, pos):
            half = HD // 2
            inv = 1.0 / THETA ** (jnp.arange(half, dtype=jnp.float32) / half)
            ang = pos[:, :, None].astype(jnp.float32) * inv
            cos = jnp.cos(ang)[:, None, :, :]
            sin = jnp.sin(ang)[:, None, :, :]
            x1, x2 = (x[..., :half], x[..., half:])
            return jnp.concatenate([x1 * cos - x2 * sin, x2 * cos + x1 * sin], axis=-1)
        Bx, Tx, _ = x.shape
        q = jnp.einsum('btd,od->bto', x, Wq).reshape(Bx, Tx, H, HD).transpose(0, 2, 1, 3)
        k = jnp.einsum('btd,od->bto', x, Wk).reshape(Bx, Tx, G, HD).transpose(0, 2, 1, 3)
        v = jnp.einsum('btd,od->bto', x, Wv).reshape(Bx, Tx, G, HD).transpose(0, 2, 1, 3)
        q = _rms(q, q_norm_scale)
        k = _rms(k, k_norm_scale)
        pos = kv_lens[:, None] + jnp.arange(Tx, dtype=jnp.int32)
        q = _rope(q, pos)
        k = _rope(k, pos)
        slot = pos // BLOCK
        off = pos % BLOCK
        blk = jnp.take_along_axis(block_tables, slot, axis=1)
        k_blocks = k_blocks.at[blk, :, off, :].set(k.transpose(0, 2, 1, 3))
        v_blocks = v_blocks.at[blk, :, off, :].set(v.transpose(0, 2, 1, 3))
        k_all = k_blocks[block_tables].transpose(0, 2, 1, 3, 4).reshape(Bx, G, -1, HD)
        v_all = v_blocks[block_tables].transpose(0, 2, 1, 3, 4).reshape(Bx, G, -1, HD)
        S = k_all.shape[2]
        qg = q.reshape(Bx, G, GSZ, Tx, HD)
        scores = jnp.einsum('bghtd,bgsd->bghts', qg, k_all) * SCALE
        kpos = jnp.arange(S, dtype=jnp.int32)
        allowed = (kpos[None, None, :] <= pos[:, :, None]) & (kpos[None, None, :] > pos[:, :, None] - WINDOW)
        scores = jnp.where(allowed[:, None, None, :, :], scores, -jnp.inf)
        p = jax.nn.softmax(scores, axis=-1)
        o = jnp.einsum('bghts,bgsd->bghtd', p, v_all).reshape(Bx, H, Tx, HD)
        o = o.transpose(0, 2, 1, 3).reshape(Bx, Tx, H * HD)
        return jnp.einsum('bto,do->btd', o, Wo)

    def _L3_cond_ref(x, subjects, weights, bias):
        import jax, jax.numpy as jnp
        import numpy as np
        B, C, T = (64, 64, 512)
        D, N = (64, 8)
        w = weights[subjects]
        b = bias[subjects]
        out = jnp.einsum('bct,bcd->bdt', x, w)
        out = out + b[:, :, None]
        return out
    x = x + _L0_cond_ref(x, itok_B_0_15, L0_cond_W, L0_cond_b)
    x = x + _L1_cond_ref(x, L1_cond_W, L1_cond_A, L1_cond_Bm, L1_cond_scalings, itok_B_0_6)
    x = x + _L2_cond_ref(x, L2_cond_Wq, L2_cond_Wk, L2_cond_Wv, L2_cond_Wo, L2_cond_q_norm_scale, L2_cond_k_norm_scale, L2_cond_k_blocks, L2_cond_v_blocks, itok_Bx257_0_4111, itok_B_37_3939)
    x = x + _L3_cond_ref(x, itok_B_0_7, L3_cond_weights, fside_8xS_0)
    return x

_drawn_inputs = setup_inputs


def setup_inputs(seed=0):
    import zlib

    import numpy as np

    out = dict(_drawn_inputs(seed))
    spreads = {'L0_cond_b': (0.10000000149011612, 0.6), 'L1_cond_scalings': (1.0, 0.6)}
    factors = {'L2_cond_q_norm_scale': 8.0,
     'L2_cond_k_norm_scale': 64.0,
     'L2_cond_k_blocks': 3.181,
     'L2_cond_Wk': 4.945}
    for name, (base, spread) in spreads.items():
        noise = np.random.default_rng([zlib.crc32(name.encode()), seed]).standard_normal(out[name].shape)
        drawn = base * np.exp(spread * noise) if base else spread * noise
        out[name] = jnp.asarray(drawn.astype(out[name].dtype))
    for name, factor in factors.items():
        out[name] = (out[name] * factor).astype(out[name].dtype)
    return out
```

```python
import concourse.bass as bass
from concourse import mybir
from contextlib import ExitStack

F32 = mybir.dt.float32
I32 = mybir.dt.int32
ALU = mybir.AluOpType
ACT = mybir.ActivationFunctionType
AX = mybir.AxisListType

NB, T, D = 64, 64, 512
P = 128
DC = D // P
NP = NB // 2
NE, NA, RANK, NS = 16, 8, 16, 8
H, G, HD = 8, 4, 64
GP = G // 2
BLK, NSLOT, NBLK = 16, 257, 4112
WIN = 256
NK = WIN + T
KVD = 2 * G * HD
WSLOT = (WIN + T) // BLK + 1
NWIN = 254
RUNS = T // BLK + 1
NRUN = NB * RUNS
EPS = 1e-6
NONE = 60000
BIG = float(2.0 ** 100)
NEGLEN = WIN + WSLOT * BLK
BITS = 9
ROWLEN = NK + 2 ** BITS


def build(nc, a):
    ctx = ExitStack()
    with ctx:
        def sb(name, shape, dt=F32):
            return ctx.enter_context(nc.sbuf_tensor(name, shape, dt))

        def sem(name):
            return ctx.enter_context(nc.semaphore(name))

        new_rows = nc.dram_tensor("new_rows", (NB * T, KVD), F32).ap()
        x2_dram = nc.dram_tensor("x2_dram", (NP, P, D), F32).ap()
        q_dram = nc.dram_tensor("q_dram", (NB, P, GP * P), F32).ap()
        writer = nc.dram_tensor("writer", (NBLK, BLK), I32).ap()
        tok_dram = nc.dram_tensor("tok_dram", (NB, RUNS * BLK), F32).ap()
        blk_dram = nc.dram_tensor("blk_dram", (NB, RUNS), F32).ap()

        ident = sb("ident", [P, P])
        band = sb("band", [P, NK])
        neg_iota = sb("neg_iota", [P, NK])
        w1 = sb("w1", [P, DC, D])
        wqkv = sb("wqkv", [P, DC, D + KVD])
        lora_a = sb("lora_a", [P, DC, P])
        lora_b = sb("lora_b", [P, D])
        wo = sb("wo", [P, DC, D])
        gains = sb("gains", [P, 2, 4, 32])
        gain_in = sb("gain_in", [P, 2, HD])
        ids_sb = sb("ids_sb", [1, 3, NB], I32)
        lora_mask = sb("lora_mask", [P, NB])
        neg_half = sb("neg_half", [P, 12])
        thr = sb("thr", [P, NB])
        idx = sb("idx", [P, NB, 5], I32)

        scol = sb("scol", [P, 24])
        icol = sb("icol", [P, 16], I32)
        kvl_row = sb("kvl_row", [P, NB], I32)
        ad_row = sb("ad_row", [P, NB], I32)
        fcols = sb("fcols", [P, 12])
        mrow = sb("mrow", [P, RUNS * BLK])
        run_row = sb("run_row", [P, NRUN])
        win_i = sb("win_i", [P, 2, WSLOT], I32)
        win_f = sb("win_f", [P, 2, WSLOT])
        tok1 = sb("tok1", [P, RUNS * BLK])
        tmp1 = sb("tmp1", [P, RUNS * BLK])
        blk_row = sb("blk_row", [P, NRUN])
        same = sb("same", [P, 3, NRUN])
        later = sb("later", [P, NRUN])
        merged = sb("merged", [P, 3, BLK])
        merged2 = sb("merged2", [P, 3, BLK])
        merged_i = sb("merged_i", [P, 3, BLK], I32)
        run_col = sb("run_col", [P, 3])
        cnt = sb("cnt", [P, 3])
        wr_idx = sb("wr_idx", [P, 3], I32)
        table_i = sb("table_i", [P, WSLOT, BLK], I32)
        rows = [sb(f"rows{i}", [P, ROWLEN]) for i in range(2)]
        shifted = sb("shifted", [P, ROWLEN])
        bits = sb("bits", [P, BITS])
        none_i = sb("none_i", [P, NBLK * BLK // P], I32)

        ring = sb("ring", [P, 4, DC * D])
        xt = sb("xt", [P, 2, DC, P])
        x_in = sb("x_in", [P, 2, D])
        bias_in = sb("bias_in", [P, 2, D])
        cs = sb("cs", [P, 2, P])
        xb = x_in
        x1 = sb("x1", [P, 2, D])
        x1t = sb("x1t", [P, 2, DC, P])
        xam = sb("xam", [P, 2, P])
        x2 = sb("x2", [P, 2, D])
        x2t = sb("x2t", [P, 2, DC, P])
        sq = sb("sq", [P, 12, HD])
        ss = sb("ss", [P, 2, 12])
        rms = sb("rms", [P, 2, 12])
        tab = sb("tab", [P, 2, 2, 4, 32])
        rot_a = sb("rot_a", [P, 12, HD])
        rot_b = sb("rot_b", [P, 12, HD])
        rot = sb("rot", [P, 12, HD])
        q_rot = sb("q_rot", [P, 2, D])
        kv_out = sb("kv_out", [P, 2, KVD])
        q_t = sb("q_t", [P, 2, 2, DC, T])

        qpad = sb("qpad", [P, 4, G, P])
        kt = sb("kt", [P, 2, GP, NK])
        big = sb("big", [P, 2 * 2 * G * NK])
        sm = big[:, 0:2 * G * NK].rearrange("p (s g n) -> p s g n", s=2, g=G)
        prob = big[:, 2 * G * NK:].rearrange("p (s g n) -> p s g n", s=2, g=G)
        tok_row = big[:, 0:NRUN * BLK].rearrange("p (r o) -> p r o", o=BLK)
        mask = sb("mask", [P, 2, NK])
        neg_max = sb("neg_max", [P, 2, G])
        row_sum = sb("row_sum", [P, 2, G])
        recip = sb("recip", [P, 2, G])
        pt = sb("pt", [P, 2, 2, 2, P])
        pt2 = sb("pt2", [T, 2, 2, P])
        ot = sb("ot", [P, 2, DC, P])
        x2_in, x3, x4 = x_in, bias_in, x1
        bd = sb("bd", [P, 2, P])
        sbias = sb("sbias", [P, 2, 1])
        idx_now = sb("idx_now", [P, 4, 5], I32)
        kv = ring[:, :, 0:3 * KVD].rearrange("p s (c n) -> p s c n", c=3)

        ps = [ctx.enter_context(nc.psum_tensor(f"ps{i}", [P, 512], F32)) for i in range(8)]
        ps_l0, ps_t2, ps_t3, ps_t1, ps_q, ps_kv, ps_la, ps_l1 = ps
        ps_s, ps_kt, ps_pt, ps_pt2, ps_o, ps_x = ps[0:2], ps[2], ps[3:5], ps[5], ps[6], ps[7]

        ld_const, ld_small, ld_cols = sem("ld_const"), sem("ld_small"), sem("ld_cols")
        cols_i, win_idx_ready, win_loaded = sem("cols_i"), sem("win_idx_ready"), sem("win_loaded")
        dv = sem("dv")
        pool_set = sem("pool_set")
        runs_stored, runs_loaded, none_stored = sem("runs_stored"), sem("runs_loaded"), sem("none_stored")
        merged_ready, writer_stored, table_loaded = sem("merged_ready"), sem("writer_stored"), sem("table_loaded")
        rows_ready, idx_t, idx_ready = sem("rows_ready"), sem("idx_t"), sem("idx_ready")
        ld_in = [sem(f"ld_in{i}") for i in range(2)]
        ld_w0 = [sem(f"ld_w0{i}") for i in range(4)]
        l0_done, t1_done, la_done, h_done = sem("l0_done"), sem("t1_done"), sem("la_done"), sem("h_done")
        t2_done, qkv_done, t3_done = sem("t2_done"), sem("qkv_done"), sem("t3_done")
        x1_ready, xam_ready, x2_ready = sem("x1_ready"), sem("xam_ready"), sem("x2_ready")
        ss_ready, ab_ready = sem("ss_ready"), sem("ab_ready")
        x1t_ready, x2t_ready, qt_ready, sqv_ready = sem("x1t_ready"), sem("x2t_ready"), sem("qt_ready"), sem("sqv_ready")
        xb_ready, tab_ready, rms_a, rms_ready = sem("xb_ready"), sem("tab_ready"), sem("rms_a"), sem("rms_ready")
        rot_sum, rot_ready = sem("rot_sum"), sem("rot_ready")
        st_x2 = [sem(f"st_x2{i}") for i in range(2)]
        st_kv = [sem(f"st_kv{i}") for i in range(2)]
        st_q = [sem(f"st_q{i}") for i in range(2)]
        ld_q = [sem(f"ld_q{i}") for i in range(4)]
        ld_pair = [sem(f"ld_pair{i}") for i in range(2)]
        idx_copied = sem("idx_copied")
        g_old = [sem(f"g_old{i}") for i in range(4)]
        g_new = [sem(f"g_new{i}") for i in range(4)]
        s_done, kt_done, pt_done, pv_done = sem("s_done"), sem("kt_done"), sem("pt_done"), sem("pv_done")
        wo_done, l3_done = sem("wo_done"), sem("l3_done")
        mask_ready, sm_ready, recip_ready = sem("mask_ready"), sem("sm_ready"), sem("recip_ready")
        pt_ready, pt2_ready, ot_ready = sem("pt_ready"), sem("pt2_ready"), sem("ot_ready")
        x3_ready, x4_ready = sem("x3_ready"), sem("x4_ready")
        e_ready, kt_ready, prob_ready = sem("e_ready"), sem("kt_ready"), sem("prob_ready")
        st_out = [sem(f"st_out{i}") for i in range(2)]

        SMALL_DMAS = 11
        CONST_DMAS = 10
        IN_DMAS = 6
        PAIR_DMAS = 5

        def loop(eng, step, slots, first, end, last):
            for n in range(first):
                step(n, n // slots, n % slots)
            with eng.Fori(first // slots, last // slots) as j:
                for s in range(slots):
                    step(j * slots + s, j, s)
            for n in range(last, end):
                step(n, n // slots, n % slots)

        def on(n, lag, count):
            return not isinstance(n, int) or 0 <= n - lag < count

        def wait(eng, semaphore, value):
            if not isinstance(value, int) or value > 0:
                eng.wait_ge(semaphore, value)

        waits_passed = {"pool": sem("pool_waits_passed"), "dve": sem("dve_waits_passed")}

        def wait_alone(eng, name, semaphore, value):
            wait(eng, semaphore, value)
            if not isinstance(value, int):
                eng.sem_inc(waits_passed[name], 1)

        block = ctx.enter_context(nc.Block())

        @block.sync
        def _(sp):
            sp.dma_start(ids_sb[:, :, :], a["ids"]).then_inc(ld_small, 16)
            for h in range(2):
                sp.dma_start(icol[T * h:T * h + T, 0:1], a["kvl"].rearrange("(b o) -> b o", o=1)).then_inc(ld_small, 16)
            sp.dma_start(fcols[:, :], a["fcols"]).then_inc(ld_small, 16)
            sp.dma_start(mrow[:, :], a["mrow"]).then_inc(ld_small, 16)
            sp.dma_start(run_row[:, :], a["runrow"]).then_inc(ld_small, 16)
            sp.dma_start(kvl_row[:, :], a["kvl"].partition_broadcast(P)).then_inc(ld_small, 16)
            sp.dma_start(ad_row[:, :], a["adapter"].partition_broadcast(P)).then_inc(ld_small, 16)
            sp.dma_start(scol[:, 0:1], a["scal"]).then_inc(ld_small, 16)
            sp.dma_start(gain_in[:, 0, :], a["qn"].partition_broadcast(P)).then_inc(ld_small, 16)
            sp.dma_start(gain_in[:, 1, :], a["kn"].partition_broadcast(P)).then_inc(ld_small, 16)
            sp.wait_ge(ld_small, SMALL_DMAS * 16)

            def load_in(k, j, s):
                wait(sp, l0_done, k - 1)
                wait(sp, x1_ready, k - 1)
                wait(sp, tab_ready, k - 1)
                sp.dma_start(xt[:, s, :, :], a["xt"][bass.ds(k, 1)].rearrange("o p c t -> (o p) c t")).then_inc(ld_in[s], 16)
                sp.dma_start(x_in[:, s, :], a["x"][bass.ds(k, 1)].rearrange("o p d -> (o p) d")).then_inc(ld_in[s], 16)
                for h in range(2):
                    e = sp.value_load(ids_sb[0:1, 0, bass.ds(k * 2 + h, 1)], min_val=0, max_val=NE - 1)
                    sp.dma_start(ring[:, 2 * s + h, :], a["w0"][bass.ds(e, 1)].rearrange("o p n -> (o p) n")).then_inc(
                        ld_w0[2 * s + h], 16)
                    sp.dma_start(bias_in[T * h:T * h + T, s, :], a["b0"][bass.ds(e, 1)].rearrange(
                        "o d -> (o d)").partition_broadcast(T)).then_inc(ld_in[s], 16)
                    p0 = sp.value_load(ids_sb[0:1, 2, bass.ds(k * 2 + h, 1)], min_val=0, max_val=NSLOT * BLK - T)
                    sp.dma_start(cs[T * h:T * h + T, s, :], a["rope"][bass.ds(p0, T), :]).then_inc(ld_in[s], 16)

            load_in(0, 0, 0)
            sp.dma_start(ident[:, :], a["ident"]).then_inc(ld_const, 16)
            sp.dma_start(w1[:, :, :], a["w1"]).then_inc(ld_const, 16)
            sp.dma_start(lora_a[:, :, :], a["la"]).then_inc(ld_const, 16)
            sp.dma_start(lora_b[:, :], a["lb"]).then_inc(ld_const, 16)
            sp.dma_start(wqkv[:, :, 0:D], a["wq"]).then_inc(ld_const, 16)
            sp.dma_start(wqkv[:, :, D:D + 256], a["wk"]).then_inc(ld_const, 16)
            sp.dma_start(wqkv[:, :, D + 256:], a["wv"]).then_inc(ld_const, 16)
            load_in(1, 0, 1)
            sp.dma_start(wo[:, :, :], a["wo"]).then_inc(ld_const, 16)
            sp.dma_start(band[:, :], a["band"]).then_inc(ld_const, 16)
            sp.dma_start(neg_iota[:, :], a["negiota"]).then_inc(ld_const, 16)
            sp.wait_ge(pool_set, 1)
            sp.dma_start(writer.rearrange("n o -> (n o)").rearrange("(p m) -> p m", p=P), none_i[:, :]).then_inc(none_stored, 16)
            sp.wait_ge(cols_i, 1)
            sp.dma_start(tok_dram, tok1[0:NB, :]).then_inc(runs_stored, 16)
            sp.dma_start(blk_dram, win_f[0:NB, 1, 0:RUNS]).then_inc(runs_stored, 16)
            sp.wait_ge(runs_stored, 32)
            sp.dma_start(tok_row.rearrange("p r o -> p (r o)"), tok_dram.rearrange("b n -> (b n)").partition_broadcast(P)).then_inc(
                runs_loaded, 16)
            sp.dma_start(blk_row[:, :], blk_dram.rearrange("b n -> (b n)").partition_broadcast(P)).then_inc(runs_loaded, 16)

            def phase_one(k, j, s):
                if on(k, 0, NP):
                    load_in(k, j, s)
                if on(k, 3, NP):
                    t = (s + 1) % 2
                    sp.wait_ge(x2_ready, k - 2)
                    sp.dma_start(x2_dram[bass.ds(k - 3, 1)].rearrange("o p d -> (o p) d"), x2[:, t, :]).then_inc(st_x2[t], 16)
                if on(k, 4, NP):
                    sp.wait_ge(rot_ready, k - 3)
                    sp.wait_ge(sqv_ready, k - 3)
                    sp.dma_start(new_rows[bass.ds((k - 4) * P, P), :], kv_out[:, s, :]).then_inc(st_kv[s], 16)

            for k in range(2, 4):
                phase_one(k, k // 2, k % 2)
            with sp.Fori(2, NP // 2) as j:
                for s in range(2):
                    phase_one(j * 2 + s, j, s)
            for k in range(NP, NP + 4):
                phase_one(k, k // 2, k % 2)

            for s in range(2):
                sp.wait_ge(st_q[s], NP // 2 * 16)
                sp.wait_ge(st_x2[s], NP // 2 * 16)
            sp.wait_ge(pool_set, 3)

            def phase_two(b, j, s):
                if on(b, 0, NB):
                    wait(sp, s_done, b * G - 3 * G if not isinstance(b, int) or b >= 4 else 0)
                    src = q_dram[bass.ds(b, 1)].rearrange("o p (g m) -> (o p) g m", g=GP)
                    for q in range(2):
                        dst = qpad[HD * q:HD * q + HD, s, :, :].rearrange("p (g q) m -> p g q m", q=2)[:, :, q, :]
                        sp.dma_start(dst, src[HD * q:HD * q + HD]).then_inc(ld_q[s], 16)
                if s % 2 == 0 and on(b, 8, NB):
                    k, t = (b // 2 - 4 if isinstance(b, int) else j * 2 + s // 2 - 4), s // 2
                    sp.wait_ge(x4_ready, k + 1)
                    sp.dma_start(a["out"][bass.ds(k, 1)].rearrange("o p d -> (o p) d"), x4[:, t, :]).then_inc(st_out[t], 16)
                if s % 2 == 0 and on(b, 0, NB):
                    k, t = (b // 2 if isinstance(b, int) else j * 2 + s // 2), s // 2
                    wait(sp, x4_ready, k - 1)
                    sp.dma_start(x2_in[:, t, :], x2_dram[bass.ds(k, 1)].rearrange("o p d -> (o p) d")).then_inc(ld_pair[t], 16)
                    for h in range(2):
                        u = sp.value_load(ids_sb[0:1, 1, bass.ds(k * 2 + h, 1)], min_val=0, max_val=NS - 1)
                        sp.dma_start(bd[T * h:T * h + T, t, T * h:T * h + T],
                                     a["w3"][bass.ds(u, 1)].rearrange("o c d -> (o c) d")).then_inc(ld_pair[t], 16)
                        sp.dma_start(sbias[T * h:T * h + T, t, :],
                                     a["b3"][bass.ds(u, 1)].rearrange("o d n -> (o d) n")).then_inc(ld_pair[t], 16)

            loop(sp, phase_two, 4, 8, NB + 8, NB)
            for t in range(2):
                sp.wait_ge(st_out[t], NP // 2 * 16)
                sp.wait_ge(st_kv[t], NP // 2 * 16)
            sp.wait_ge(writer_stored, 48)
            sp.wait_ge(none_stored, 16)

        @block.gpsimd
        def _(pool):
            nc.gpsimd.memset(none_i[:, :], NONE).then_inc(pool_set, 1)
            nc.gpsimd.memset(neg_half[:, :], -0.5).then_inc(pool_set, 1)
            nc.gpsimd.memset(bd[:, :, :], 0.0)
            nc.gpsimd.memset(qpad[:, :, :, :], 0.0).then_inc(pool_set, 1)
            pool.wait_ge(win_idx_ready, 1)
            for w in range(2):
                pool.indirect_dma_start(out=win_i[:, w, :], out_offset=None, in_=a["windows"],
                                        in_offset=bass.IndirectOffsetOnAxis(ap=icol[:, 4 + w:5 + w], axis=0)).then_inc(win_loaded, 16)
            pool.wait_ge(none_stored, 16)
            pool.wait_ge(merged_ready, 1)
            for m in range(3):
                n = P if m < 2 else NB
                pool.indirect_dma_start(out=writer, out_offset=bass.IndirectOffsetOnAxis(ap=wr_idx[0:n, m:m + 1], axis=0),
                                        in_=merged_i[0:n, m, :], in_offset=None,
                                        bounds_check=NBLK - 1, oob_is_err=False).then_inc(writer_stored, 16)
            pool.wait_ge(writer_stored, 48)
            for w in range(WSLOT):
                pool.indirect_dma_start(out=table_i[:, w, :], out_offset=None, in_=writer,
                                        in_offset=bass.IndirectOffsetOnAxis(ap=win_i[:, 0, w:w + 1], axis=0)).then_inc(table_loaded, 16)

            def phase_one(k, j, s):
                if on(k, 0, NP):
                    pool.wait_ge(ld_in[s], IN_DMAS * 16 * (j + 1))
                    wait(pool, x1_ready, k - 1)
                    nc.gpsimd.tensor_tensor(xb[:, s, :], x_in[:, s, :], bias_in[:, s, :], ALU.add).then_inc(xb_ready, 1)
                    wait(pool, ab_ready, k - 1)
                    nc.gpsimd.tensor_tensor(tab[:, s, :, :, :].rearrange("p w f n -> p w (f n)"), gains[:, :, :, :].rearrange("p w f n -> p w (f n)"),
                                            cs[:, s, :].unsqueeze(1).to_broadcast([P, 2, P]), ALU.mult).then_inc(tab_ready, 1)
                if on(k, 2, NP):
                    pool.wait_ge(ss_ready, k - 1)
                    nc.gpsimd.tensor_tensor(rms[:, s, :], ss[:, s, :], neg_half[:, :], ALU.pow).then_inc(rms_ready, 1)
                    pool.wait_ge(ab_ready, k - 1)
                    wait(pool, rot_ready, k - 2)
                    nc.gpsimd.tensor_tensor(rot[:, :, :], rot_a[:, :, :], rot_b[:, :, :], ALU.add).then_inc(rot_sum, 1)
                    pool.wait_ge(rot_sum, k - 1)
                    pool.wait_ge(rms_ready, k - 1)
                    wait(pool, t3_done, k - 3)
                    wait(pool, st_kv[s], 16 * (j - 1))
                    nc.gpsimd.tensor_tensor(q_rot[:, s, :].rearrange("p (g d) -> p g d", d=HD), rot[:, 0:8, :],
                                            rms[:, s, 0:8].unsqueeze(2).to_broadcast([P, 8, HD]), ALU.mult)
                    nc.gpsimd.tensor_tensor(kv_out[:, s, 0:256].rearrange("p (g d) -> p g d", d=HD), rot[:, 8:12, :],
                                            rms[:, s, 8:12].unsqueeze(2).to_broadcast([P, 4, HD]), ALU.mult).then_inc(rot_ready, 1)

            pool.wait_ge(cols_i, 1)
            loop(pool, phase_one, 2, 4, NP + 2, NP)

            for s in range(2):
                pool.wait_ge(st_kv[s], NP // 2 * 16)
            pool.wait_ge(idx_ready, 1)
            pool.wait_ge(l0_done, NP)

            def gather(b, j, s):
                wait_alone(pool, "pool", pv_done, 2 * b - 6 if not isinstance(b, int) or b >= 4 else 0)
                nc.gpsimd.tensor_copy(idx_now[:, s, :], idx[:, bass.ds(b, 1), :].rearrange("p o n -> p (o n)")).then_inc(idx_copied, 1)
                wait_alone(pool, "pool", idx_copied, b + 1)
                for c in range(2):
                    pool.indirect_dma_start(out=kv[:, s, c, :], out_offset=None, in_=a["kvrows"],
                                            in_offset=bass.IndirectOffsetOnAxis(ap=idx_now[:, s, c:c + 1], axis=0)).then_inc(g_old[s], 16)
                pool.indirect_dma_start(out=kv[0:T, s, 2, :], out_offset=None, in_=new_rows,
                                        in_offset=bass.IndirectOffsetOnAxis(ap=idx_now[0:T, s, 4:5], axis=0)).then_inc(g_old[s], 16)
                wait_alone(pool, "pool", g_old[s], 48 * (j + 1))
                for c in range(2):
                    pool.indirect_dma_start(out=kv[:, s, c, :], out_offset=None, in_=new_rows,
                                            in_offset=bass.IndirectOffsetOnAxis(ap=idx_now[:, s, 2 + c:3 + c], axis=0),
                                            bounds_check=NB * T - 1, oob_is_err=False).then_inc(g_new[s], 16)

            gather(0, 0, 0)
            gather(1, 0, 1)

            def phase_two(b, j, s):
                if on(b, -2, NB):
                    gather(b + 2, j + (s >= 2), (s + 2) % 4)
                wait_alone(pool, "pool", recip_ready, b + 1)
                for g in range(G):
                    last = nc.gpsimd.tensor_scalar(prob[:, s % 2, g, :], prob[:, s % 2, g, :], recip[:, s % 2, g:g + 1], 1.0,
                                                   ALU.mult, ALU.mult).then_inc(prob_ready, 1)

            loop(pool, phase_two, 4, 4, NB, NB - 4)

        @block.tensor
        def _(pe):
            pe.wait_ge(ld_const, CONST_DMAS * 16)

            def phase_one(k, j, s):
                r = 1 - s
                if on(k, 0, NP):
                    pe.wait_ge(ld_in[s], IN_DMAS * 16 * (j + 1))
                    pe.wait_ge(ld_w0[2 * s], 16 * (j + 1))
                    pe.wait_ge(ld_w0[2 * s + 1], 16 * (j + 1))
                    wait(pe, x1_ready, k)
                    for c in range(DC):
                        for h in range(2):
                            last = nc.tensor.matmul(ps_l0[T * h:T * h + T, :], xt[:, s, c, T * h:T * h + T],
                                                    ring[:, 2 * s + h, c * D:(c + 1) * D], start=(c == 0), stop=(c == DC - 1))
                    last.then_inc(l0_done, 1)
                if on(k, 1, NP):
                    pe.wait_ge(x2_ready, k)
                    wait(pe, x2t_ready, k - 1)
                    for c in range(DC):
                        last = nc.tensor.transpose(ps_t2[:, c * P:(c + 1) * P], x2[:, r, c * P:(c + 1) * P], ident[:, :])
                    last.then_inc(t2_done, 1)
                if on(k, 2, NP):
                    pe.wait_ge(rot_ready, k - 1)
                    wait(pe, qt_ready, k - 2)
                    for c in range(DC):
                        last = nc.tensor.transpose(ps_t3[:, c * P:(c + 1) * P], q_rot[:, s, c * P:(c + 1) * P], ident[:, :])
                    last.then_inc(t3_done, 1)
                if on(k, 0, NP):
                    pe.wait_ge(x1_ready, k + 1)
                    wait(pe, x1t_ready, k)
                    for c in range(DC):
                        last = nc.tensor.transpose(ps_t1[:, c * P:(c + 1) * P], x1[:, s, c * P:(c + 1) * P], ident[:, :])
                    last.then_inc(t1_done, 1)
                if on(k, 1, NP):
                    pe.wait_ge(x2t_ready, k)
                    wait(pe, ab_ready, k - 1)
                    wait(pe, sqv_ready, k - 1)
                    for c in range(DC):
                        nc.tensor.matmul(ps_q[:, :], x2t[:, r, c, :], wqkv[:, c, 0:D], start=(c == 0), stop=(c == DC - 1))
                    for c in range(DC):
                        last = nc.tensor.matmul(ps_kv[:, :], x2t[:, r, c, :], wqkv[:, c, D:D + KVD], start=(c == 0), stop=(c == DC - 1))
                    last.then_inc(qkv_done, 1)
                if on(k, 0, NP):
                    pe.wait_ge(x1t_ready, k + 1)
                    wait(pe, xam_ready, k)
                    for c in range(DC):
                        last = nc.tensor.matmul(ps_la[:, 0:P], lora_a[:, c, :], x1t[:, s, c, :], start=(c == 0), stop=(c == DC - 1))
                    last.then_inc(la_done, 1)
                    wait(pe, x2_ready, k)
                    for c in range(DC):
                        nc.tensor.matmul(ps_l1[:, :], x1t[:, s, c, :], w1[:, c, :], start=(c == 0), stop=False)
                    pe.wait_ge(xam_ready, k + 1)
                    nc.tensor.matmul(ps_l1[:, :], xam[:, s, :], lora_b[:, :], start=False, stop=True).then_inc(h_done, 1)

            loop(pe, phase_one, 2, 4, NP + 2, NP)

            pe.wait_ge(rows_ready, 1)
            pe.wait_ge(x1t_ready, NP)
            for c in range(3):
                n = P if c < 2 else T
                last = nc.tensor.transpose(ps_t1[0:n, c * P:(c + 1) * P], rows[1][:, c * P:c * P + n], ident[:, :])
            last.then_inc(idx_t, 1)
            pe.wait_ge(idx_ready, 1)
            pe.wait_ge(x2_ready, NP)
            pe.wait_ge(ab_ready, NP)
            pe.wait_ge(sqv_ready, NP)
            pe.wait_ge(qt_ready, NP)

            def transpose_keys(b, j, s, p):
                if p == 0:
                    pe.wait_ge(g_old[s], 48 * (j + 1))
                    pe.wait_ge(g_new[s], 32 * (j + 1))
                wait(pe, kt_ready, 2 * b + p)
                for c in range(3):
                    n = P if c < 2 else T
                    last = nc.tensor.transpose(ps_kt[:, c * P:c * P + n], kv[0:n, s, c, p * P:(p + 1) * P], ident[0:n, 0:n])
                last.then_inc(kt_done, 1)

            for p in range(GP):
                transpose_keys(0, 0, 0, p)

            def phase_two(b, j, s):
                r = (s - 1) % 4
                pair_j, pair_s = (j if s == 3 else j - 1), 0 if s == 3 else 1
                turn = s % 2 == 1 and on(b, 3, NB)

                def scores(g):
                    wait(pe, sm_ready, G * b + g - 1)
                    if g % 2 == 0:
                        pe.wait_ge(kt_ready, 2 * b + g // 2 + 1)
                    if g == 0:
                        pe.wait_ge(ld_q[s], 32 * (j + 1))
                    nc.tensor.matmul(ps_s[g % 2][:, 0:NK], qpad[:, s, g, :], kt[:, s % 2, g // 2, :],
                                     start=True, stop=True).then_inc(s_done, 1)

                def transpose_probs(p):
                    pe.wait_ge(prob_ready, G * b - G + 2 * p + 2)
                    wait(pe, pt_ready, 2 * b - 3 + p)
                    wait(pe, pt2_ready, 2 * b - 3 + p)
                    for q in range(2):
                        for c in range(3):
                            n = P if c < 2 else T
                            dst = ps_pt[p][:, (q * 2 + c) * P:(q * 2 + c + 1) * P] if c < 2 else \
                                ps_pt2[0:T, (p * 2 + q) * P:(p * 2 + q + 1) * P]
                            last = nc.tensor.transpose(dst, prob[:, r % 2, 2 * p + q, c * P:c * P + n], ident[:, :])
                    last.then_inc(pt_done, 1)

                def values(p):
                    pe.wait_ge(pt_ready, 2 * b - 1 + p)
                    pe.wait_ge(pt2_ready, 2 * b - 1 + p)
                    wait(pe, ot_ready, 2 * b - 3 + p)
                    for c in range(3):
                        n = P if c < 2 else T
                        for q in range(2):
                            rhs = pt[:, p, q, c, :] if c < 2 else pt2[:, p, q, :]
                            v0 = G * HD + (2 * p + q) * HD
                            last = nc.tensor.matmul(ps_o[HD * q:HD * q + HD, p * P:(p + 1) * P], kv[0:n, r, c, v0:v0 + HD], rhs,
                                                    start=(c == 0), stop=(c == 2))
                    last.then_inc(pv_done, 1)

                if on(b, 0, NB):
                    scores(0)
                    scores(1)
                if on(b, -1, NB):
                    transpose_keys(b + 1, j + (s == 3), (s + 1) % 4, 0)
                if on(b, 0, NB):
                    scores(2)
                if on(b, -1, NB):
                    transpose_keys(b + 1, j + (s == 3), (s + 1) % 4, 1)
                if on(b, 0, NB):
                    scores(3)
                if on(b, 1, NB):
                    transpose_probs(0)
                if turn:
                    pair = (b - 3) // 2 if isinstance(b, int) else j * 2 + (0 if s == 3 else -1)
                    pe.wait_ge(ot_ready, 4 * pair + 4)
                    wait(pe, x4_ready, pair)
                    for c in range(DC):
                        last = nc.tensor.matmul(ps_x[:, :], ot[:, pair_s, c, :], wo[:, c, :], start=(c == 0), stop=(c == DC - 1))
                    last.then_inc(wo_done, 1)
                if on(b, 1, NB):
                    values(0)
                    transpose_probs(1)
                if turn:
                    pe.wait_ge(x3_ready, pair + 1)
                    pe.wait_ge(ld_pair[pair_s], PAIR_DMAS * 16 * (pair_j + 1))
                    nc.tensor.matmul(ps_x[:, :], bd[:, pair_s, :], x3[:, pair_s, :], start=True, stop=True).then_inc(l3_done, 1)
                if on(b, 1, NB):
                    values(1)

            loop(pe, phase_two, 4, 4, NB + 2, NB - 4)

        @block.scalar
        def _(act):
            def phase_one(k, j, s):
                r = 1 - s
                if on(k, 1, NP):
                    act.wait_ge(t2_done, k)
                    wait(act, qkv_done, k - 2)
                    nc.scalar.activation(x2t[:, r, :, :].rearrange("p c t -> p (c t)"), ps_t2[:, :], ACT.Copy).then_inc(x2t_ready, 1)
                if on(k, 2, NP):
                    act.wait_ge(t3_done, k - 1)
                    wait(act, st_q[s], 16 * j - 16)
                    nc.scalar.activation(q_t[:, s, :, :, :], ps_t3[:, :].rearrange("p (c h t) -> p h c t", c=DC, h=2),
                                         ACT.Copy).then_inc(qt_ready, 1)
                if on(k, 0, NP):
                    act.wait_ge(t1_done, k + 1)
                    wait(act, h_done, k - 1)
                    nc.scalar.activation(x1t[:, s, :, :].rearrange("p c t -> p (c t)"), ps_t1[:, :], ACT.Copy).then_inc(x1t_ready, 1)
                if on(k, 2, NP):
                    act.wait_ge(qt_ready, k - 1)
                    act.dma_start(q_dram[bass.ds(k * 2 - 4, 2)].rearrange("h p n -> p h n"),
                                  q_t[:, s, :, :, :].rearrange("p h c t -> p h (c t)")).then_inc(st_q[s], 16)
                if on(k, 1, NP):
                    act.wait_ge(qkv_done, k)
                    wait(act, ss_ready, k - 1)
                    nc.scalar.activation(sq[:, 0:8, :].rearrange("p g d -> p (g d)"), ps_q[:, :], ACT.Square)
                    nc.scalar.activation(sq[:, 8:12, :].rearrange("p g d -> p (g d)"), ps_kv[:, 0:256], ACT.Square)
                    wait(act, st_kv[r], 16 * (j - 1 + s))
                    nc.scalar.activation(kv_out[:, r, 256:512], ps_kv[:, 256:512], ACT.Copy).then_inc(sqv_ready, 1)

            loop(act, phase_one, 2, 4, NP + 2, NP)

            def copy_keys(b, s, p):
                act.wait_ge(kt_done, 2 * b + p + 1)
                wait(act, s_done, G * b - G if not isinstance(b, int) or b >= 2 else 0)
                nc.scalar.activation(kt[:, s % 2, p, :], ps_kt[:, 0:NK], ACT.Copy).then_inc(kt_ready, 1)

            for p in range(GP):
                copy_keys(0, 0, p)

            def phase_two(b, j, s):
                def exps(g):
                    act.wait_ge(sm_ready, G * b + g + 1)
                    wait(act, pt_done, 2 * b - 2)
                    nc.scalar.activation(prob[:, s % 2, g, :], sm[:, s % 2, g, :], ACT.Exp, bias=neg_max[:, s % 2, g:g + 1],
                                         scale=-1.0, accum_out=row_sum[:, s % 2, g:g + 1]).then_inc(e_ready, 1)

                if on(b, 0, NB):
                    exps(0)
                if on(b, -1, NB):
                    copy_keys(b + 1, s + 1, 0)
                if on(b, 0, NB):
                    exps(1)
                    exps(2)
                if on(b, -1, NB):
                    copy_keys(b + 1, s + 1, 1)
                if on(b, 0, NB):
                    exps(3)
                if on(b, 1, NB):
                    for p in range(GP):
                        act.wait_ge(pt_done, 2 * b - 1 + p)
                        wait(act, pv_done, 2 * b - 3 + p)
                        nc.scalar.activation(pt2[:, p, :, :].rearrange("p q t -> p (q t)"),
                                             ps_pt2[0:T, p * 2 * P:(p + 1) * 2 * P], ACT.Copy).then_inc(pt2_ready, 1)

            loop(act, phase_two, 4, 4, NB + 1, NB - 4)

        @block.vector
        def _(dve):
            chain = [0]

            def link(ins):
                chain[0] += 1
                ins.then_inc(dv, 1)
                dve.wait_ge(dv, chain[0])

            V = nc.vector
            BCOL, ACOL, BROW, R0 = 0, 1, 2, 3
            dve.wait_ge(ld_small, SMALL_DMAS * 16)
            link(V.tensor_scalar(icol[:, 1:2], icol[:, 0:1], BLK - 1, None, ALU.bitwise_and))
            link(V.tensor_scalar(icol[:, 2:3], icol[:, 0:1], float(WIN), 0.0, ALU.subtract, ALU.max))
            link(V.tensor_scalar(icol[:, 3:4], icol[:, 2:3], 4, None, ALU.logical_shift_right))
            link(V.tensor_scalar(icol[:, 6:7], icol[:, 0:1], 4, None, ALU.logical_shift_right))
            link(V.tensor_tensor(icol[:, 4:5], icol[:, 3:4], fcols[:, BROW:BROW + 1], ALU.add))
            V.tensor_tensor(icol[:, 5:6], icol[:, 6:7], fcols[:, BROW:BROW + 1], ALU.add).then_inc(win_idx_ready, 1)
            link(V.tensor_scalar(scol[:, 1:2], icol[:, 0:1], float(WIN), None, ALU.is_ge))
            link(V.tensor_tensor(scol[:, 2:3], scol[:, 1:2], icol[:, 1:2], ALU.mult))
            link(V.scalar_tensor_tensor(icol[:, 7:8], icol[:, 0:1], float(WIN), scol[:, 2:3], ALU.min, ALU.add))
            for n in range(BITS):
                link(V.tensor_scalar(icol[:, 8:9], icol[:, 7:8], n, 1, ALU.logical_shift_right, ALU.bitwise_and))
                link(V.tensor_copy(bits[:, n:n + 1], icol[:, 8:9]))
            link(V.tensor_copy(scol[:, 3:4], icol[:, 1:2]))
            link(V.tensor_scalar(tmp1[:, :], mrow[:, :], scol[:, 3:4], None, ALU.subtract))
            link(V.tensor_scalar(tok1[:, :], tmp1[:, :], fcols[:, BCOL:BCOL + 1], None, ALU.add))
            link(V.scalar_tensor_tensor(tok1[:, :], tmp1[:, :], 0.0, tok1[:, :], ALU.is_ge, ALU.mult))
            link(V.scalar_tensor_tensor(tok1[:, :], tmp1[:, :], float(T - 1), tok1[:, :], ALU.is_le, ALU.mult))
            link(V.tensor_scalar(lora_mask[:, :], ad_row[:, :], fcols[:, ACOL:ACOL + 1], scol[:, 0:1], ALU.is_equal, ALU.mult))
            link(V.tensor_scalar(thr[:, :], kvl_row[:, :], -BIG, BIG * WIN, ALU.mult, ALU.add))
            link(V.tensor_scalar(gain_in[:, :, :], gain_in[:, :, :], 1.0, None, ALU.add))
            for w, g in ((0, -1.0 / 16.0), (1, 1.0)):
                for f, half, sign in ((0, 0, 1.0), (1, 1, 1.0), (2, 1, -1.0), (3, 0, 1.0)):
                    link(V.tensor_scalar(gains[:, w, f, :], gain_in[:, w, 32 * half:32 * half + 32], g * sign, None, ALU.mult))
            dve.wait_ge(win_loaded, 32)
            link(V.tensor_copy(win_f[:, :, :], win_i[:, :, :]))
            V.tensor_copy(scol[:, 4:5], scol[:, 3:4]).then_inc(cols_i, 1)
            for m in range(3):
                for h in range(2 if m < 2 else 1):
                    link(V.tensor_copy(run_col[T * h:T * h + T, m:m + 1], win_f[T * h:T * h + T, 1, 2 * m + h:2 * m + h + 1]))
            dve.wait_ge(runs_loaded, 32)
            for m in range(3):
                n = P if m < 2 else NB
                link(V.tensor_scalar(same[0:n, m, :], blk_row[0:n, :], run_col[0:n, m:m + 1], None, ALU.is_equal))
                link(V.scalar_tensor_tensor(later[0:n, :], run_row[0:n, :], fcols[0:n, R0 + m:R0 + m + 1], same[0:n, m, :],
                                            ALU.is_gt, ALU.mult, accum_out=cnt[0:n, m:m + 1]))
                for o in range(BLK):
                    link(V.tensor_tensor_reduce(later[0:n, :], same[0:n, m, :], tok_row[0:n, :, o], 1.0, 0.0, ALU.mult, ALU.max,
                                                  accum_out=merged[0:n, m, o:o + 1]))
                link(V.scalar_tensor_tensor(wr_idx[0:n, m:m + 1], cnt[0:n, m:m + 1], 8192.0, run_col[0:n, m:m + 1], ALU.mult, ALU.add))
                link(V.tensor_scalar(merged2[0:n, m, :], merged[0:n, m, :], 0.0, NONE + 1.0, ALU.is_equal, ALU.mult))
                link(V.scalar_tensor_tensor(merged_i[0:n, m, :], merged[0:n, m, :], -1.0, merged2[0:n, m, :], ALU.add, ALU.add))
            V.tensor_copy(scol[:, 4:5], scol[:, 3:4]).then_inc(merged_ready, 1)

            link(V.memset(rows[0][:, NEGLEN:], 0.0))
            link(V.tensor_scalar(win_f[:, 0, :], win_f[:, 0, :], float(BLK), None, ALU.mult))
            link(V.tensor_tensor(rows[0][0:NB, WIN:NEGLEN].rearrange("p (w o) -> p w o", o=BLK),
                                 win_f[0:NB, 0, :].unsqueeze(2).to_broadcast([NB, WSLOT, BLK]),
                                 mrow[0:NB, 0:BLK].unsqueeze(1).to_broadcast([NB, WSLOT, BLK]), ALU.add))
            dve.wait_ge(table_loaded, 16 * WSLOT)
            link(V.tensor_copy(rows[0][NB:P, WIN:NEGLEN], table_i[NB:P, :, :].rearrange("p w o -> p (w o)")))
            link(V.tensor_copy(rows[0][:, 0:WIN], rows[0][:, WIN:WIN + 1].to_broadcast([P, WIN])))
            for i, n in enumerate(reversed(range(BITS))):
                size = NK + 2 ** n - 1
                src, dst = rows[i % 2], rows[(i + 1) % 2]
                link(V.tensor_tensor(shifted[:, 0:size], src[:, 2 ** n:2 ** n + size], src[:, 0:size], ALU.subtract))
                link(V.scalar_tensor_tensor(dst[:, 0:size], shifted[:, 0:size], bits[:, n:n + 1], src[:, 0:size], ALU.mult, ALU.add))
            V.tensor_copy(scol[:, 4:5], scol[:, 3:4]).then_inc(rows_ready, 1)

            def phase_one(k, j, s):
                r = 1 - s
                if on(k, 0, NP):
                    dve.wait_ge(l0_done, k + 1)
                    dve.wait_ge(xb_ready, k + 1)
                    wait(dve, t1_done, k - 1)
                    wait(dve, x2_ready, k - 1)
                    V.tensor_tensor(x1[:, s, :], ps_l0[:, :], xb[:, s, :], ALU.add).then_inc(x1_ready, 1)
                    dve.wait_ge(la_done, k + 1)
                    wait(dve, h_done, k - 1)
                    V.tensor_tensor(xam[:, s, :].rearrange("p (h t) -> p h t", h=2), ps_la[:, 0:P].rearrange("p (h t) -> p h t", h=2),
                                    lora_mask[:, bass.ds(k * 2, 2)].unsqueeze(2).to_broadcast([P, 2, T]), ALU.mult).then_inc(xam_ready, 1)
                if on(k, 1, NP):
                    dve.wait_ge(sqv_ready, k)
                    wait(dve, rms_ready, k - 2)
                    V.tensor_reduce(ss[:, r, :], sq[:, :, :], AX.X, ALU.add).then_inc(rms_a, 1)
                    dve.wait_ge(rms_a, k)
                    V.tensor_scalar(ss[:, r, :], ss[:, r, :], 1.0 / HD, EPS, ALU.mult, ALU.add).then_inc(ss_ready, 1)
                    dve.wait_ge(tab_ready, k)
                    wait(dve, rot_sum, k - 1)
                    for w, src, g0, n in ((0, ps_q, 0, 8), (1, ps_kv, 8, 4)):
                        u = src[:, 0:n * HD].rearrange("p (g d) -> p g d", d=HD)
                        t = tab[:, r, w, :, :]
                        V.tensor_tensor(rot_a[:, g0:g0 + n, :], u, t[:, 0:2, :].rearrange("p f n -> p (f n)").unsqueeze(1).to_broadcast(
                            [P, n, HD]), ALU.mult)
                        V.tensor_tensor(rot_b[:, g0:g0 + n, 0:32], u[:, :, 32:64], t[:, 2, :].unsqueeze(1).to_broadcast([P, n, 32]), ALU.mult)
                        last = V.tensor_tensor(rot_b[:, g0:g0 + n, 32:64], u[:, :, 0:32], t[:, 3, :].unsqueeze(1).to_broadcast([P, n, 32]),
                                               ALU.mult)
                    last.then_inc(ab_ready, 1)
                if on(k, 0, NP):
                    dve.wait_ge(h_done, k + 1)
                    wait(dve, t2_done, k - 1)
                    wait(dve, st_x2[s], 16 * j)
                    V.tensor_tensor(x2[:, s, :], ps_l1[:, :], x1[:, s, :], ALU.add).then_inc(x2_ready, 1)

            loop(dve, phase_one, 2, 4, NP + 2, NP)

            dve.wait_ge(idx_t, 1)
            tview = ps_t1[:, :].rearrange("p (c w b) -> p c w b", c=4, w=2)
            for c, w, col in ((0, 0, 0), (1, 0, 1), (0, 1, 2), (1, 1, 3)):
                V.tensor_copy(idx[:, :, col], tview[:, c, w, :])
            V.memset(idx[T:P, :, 4], 0)
            V.tensor_copy(idx[0:T, :, 4], tview[0:T, 2, 1, :]).then_inc(idx_ready, 1)

            def make_mask(b, s):
                wait(dve, sm_ready, G * b - G)
                V.scalar_tensor_tensor(mask[:, s % 2, :], neg_iota[:, :], thr[:, bass.ds(b, 1)], band[:, :],
                                       ALU.add, ALU.max).then_inc(mask_ready, 1)

            dve.wait_ge(ld_const, CONST_DMAS * 16)
            make_mask(0, 0)

            def phase_two(b, j, s):
                def copy_probs(p):
                    dve.wait_ge(pt_done, 2 * b - 1 + p)
                    wait(dve, pv_done, 2 * b - 3 + p)
                    V.tensor_copy(pt[:, p, :, :, :].rearrange("p q c t -> p (q c t)"), ps_pt[p][:, :]).then_inc(pt_ready, 1)

                def copy_outputs(p):
                    pair = (b - 1) // 2 if isinstance(b, int) else j * 2 + (s - 1) // 2
                    dve.wait_ge(pv_done, 2 * b - 1 + p)
                    wait(dve, wo_done, pair - 1)
                    h = (s - 1) % 2
                    V.tensor_copy(ot[:, ((s - 1) % 4) // 2, 2 * p:2 * p + 2, T * h:T * h + T],
                                  ps_o[:, p * P:(p + 1) * P].rearrange("p (c t) -> p c t", c=2)).then_inc(ot_ready, 1)

                turn = s % 2 == 1 and on(b, 3, NB)
                if turn:
                    pair = (b - 3) // 2 if isinstance(b, int) else j * 2 + (0 if s == 3 else -1)
                    pair_j, pair_s = (j if s == 3 else j - 1), 0 if s == 3 else 1
                if on(b, 0, NB):
                    dve.wait_ge(mask_ready, b + 1)
                    for g in range(G):
                        dve.wait_ge(s_done, G * b + g + 1)
                        wait_alone(dve, "dve", e_ready, G * b + g - 2 * G + 1)
                        V.tensor_tensor_reduce(sm[:, s % 2, g, :], ps_s[g % 2][:, 0:NK], mask[:, s % 2, :], 1.0, 3.0e38,
                                               ALU.add, ALU.min, accum_out=neg_max[:, s % 2, g:g + 1]).then_inc(sm_ready, 1)
                if on(b, 1, NB):
                    copy_probs(0)
                if on(b, 0, NB):
                    dve.wait_ge(e_ready, G * b + G)
                    wait(dve, prob_ready, G * b - G)
                    V.reciprocal(recip[:, s % 2, :], row_sum[:, s % 2, :]).then_inc(recip_ready, 1)
                if turn:
                    dve.wait_ge(wo_done, pair + 1)
                    dve.wait_ge(ld_pair[pair_s], PAIR_DMAS * 16 * (pair_j + 1))
                    V.tensor_tensor(x3[:, pair_s, :], ps_x[:, :], x2_in[:, pair_s, :], ALU.add).then_inc(x3_ready, 1)
                if on(b, 1, NB):
                    copy_outputs(0)
                    copy_probs(1)
                if turn:
                    dve.wait_ge(l3_done, pair + 1)
                    dve.wait_ge(x3_ready, pair + 1)
                    wait(dve, st_out[pair_s], 16 * pair_j)
                    V.scalar_tensor_tensor(x4[:, pair_s, :], ps_x[:, :], sbias[:, pair_s, 0:1], x3[:, pair_s, :],
                                           ALU.add, ALU.add).then_inc(x4_ready, 1)
                if on(b, 1, NB):
                    copy_outputs(1)
                if on(b, -1, NB):
                    make_mask(b + 1, s + 1)

            loop(dve, phase_two, 4, 8, NB + 2, NB - 4)


def kernel(x, itok_B_0_15, itok_B_0_6, itok_Bx257_0_4111, itok_B_37_3939, itok_B_0_7, fside_8xS_0, L0_cond_W, L0_cond_b,
           L1_cond_W, L1_cond_A, L1_cond_Bm, L1_cond_scalings, L2_cond_Wq, L2_cond_Wk, L2_cond_Wv, L2_cond_Wo,
           L2_cond_q_norm_scale, L2_cond_k_norm_scale, L2_cond_k_blocks, L2_cond_v_blocks, L3_cond_weights):
    import numpy as np
    import concourse.bacc as bacc
    from concourse.bass_utils import run_bass_kernel_spmd

    A = np.ascontiguousarray
    x = np.asarray(x)
    ids = np.stack([np.asarray(itok_B_0_15), np.asarray(itok_B_0_7), np.asarray(itok_B_37_3939)])[None]
    table = np.asarray(itok_Bx257_0_4111)
    padded = np.concatenate([table, np.repeat(table[:, -1:], NWIN + WSLOT - 1 - NSLOT, axis=1)], axis=1)
    windows = np.lib.stride_tricks.sliding_window_view(padded, WSLOT, axis=1)
    wq = np.asarray(L2_cond_Wq).reshape(GP, 2, 2, HD, DC, P).transpose(5, 4, 0, 2, 1, 3)
    wo = np.asarray(L2_cond_Wo).reshape(D, GP, 2, 2, HD).transpose(2, 4, 1, 3, 0)
    kvrows = np.concatenate([np.asarray(t).transpose(0, 2, 1, 3).reshape(NBLK * BLK, G * HD)
                             for t in (L2_cond_k_blocks, L2_cond_v_blocks)], axis=1)
    arrays = {
        "x": A(x.reshape(NP, P, D)),
        "xt": A(x.reshape(NP, P, P, DC).transpose(0, 2, 3, 1)),
        "ids": A(ids),
        "kvl": A(np.asarray(itok_B_37_3939)),
        "adapter": A(np.asarray(itok_B_0_6)),
        "windows": A(windows.reshape(NB * NWIN, WSLOT)),
        "scal": A(np.repeat(np.asarray(L1_cond_scalings), RANK)[:, None]),
        "qn": A(np.asarray(L2_cond_q_norm_scale)),
        "kn": A(np.asarray(L2_cond_k_norm_scale)),
        "w0": A(np.asarray(L0_cond_W).reshape(NE, P, DC * D)),
        "b0": A(np.asarray(L0_cond_b)),
        "w1": A(np.asarray(L1_cond_W).reshape(D, DC, P).transpose(2, 1, 0)),
        "la": A(np.asarray(L1_cond_A).reshape(P, DC, P).transpose(2, 1, 0)),
        "lb": A(np.asarray(L1_cond_Bm).transpose(0, 2, 1).reshape(P, D)),
        "wq": A(wq.reshape(P, DC, D)),
        "wk": A(np.asarray(L2_cond_Wk).reshape(G * HD, DC, P).transpose(2, 1, 0)),
        "wv": A(np.asarray(L2_cond_Wv).reshape(G * HD, DC, P).transpose(2, 1, 0)),
        "wo": A(wo.reshape(P, DC, D)),
        "kvrows": A(kvrows),
        "w3": A(np.asarray(L3_cond_weights)),
        "b3": A(np.asarray(fside_8xS_0)[:, :, None]),
    }
    row = np.arange(P)
    b, half = row % NB, row // NB
    i, t = np.arange(NK)[None, :], (row % T)[:, None]
    fcols = np.zeros((P, 12), np.float32)
    fcols[:, 0] = T * b + 1
    fcols[:, 1] = row // RANK
    fcols[:, 2] = b * NWIN
    for m in range(3):
        fcols[:, 3 + m] = RUNS * b + 2 * m + half
    inv = np.float32(1.0) / np.float32(10000.0) ** (np.arange(HD // 2, dtype=np.float32) / np.float32(HD // 2))
    angle = np.arange(NSLOT * BLK, dtype=np.float32)[:, None] * inv.astype(np.float32)
    cos, sin = np.cos(angle).astype(np.float32), np.sin(angle).astype(np.float32)
    arrays.update({
        "fcols": fcols,
        "mrow": A(np.broadcast_to(np.arange(RUNS * BLK, dtype=np.float32), (P, RUNS * BLK))),
        "runrow": A(np.broadcast_to(np.arange(NRUN, dtype=np.float32), (P, NRUN))),
        "ident": np.eye(P, dtype=np.float32),
        "band": np.where((i > t) & (i <= WIN + t), 0.0, BIG).astype(np.float32),
        "negiota": A(np.broadcast_to(-BIG * i, (P, NK)).astype(np.float32)),
        "rope": A(np.concatenate([cos, cos, sin, sin], axis=1)),
    })
    nc = bacc.Bacc("TRN2", target_bir_lowering=False, num_devices=1)
    aps = {n: nc.dram_tensor("in_" + n, v.shape, mybir.dt.from_np(v.dtype), kind="ExternalInput").ap() for n, v in arrays.items()}
    aps["out"] = nc.dram_tensor("out", (NP, P, D), F32, kind="ExternalOutput").ap()
    build(nc, aps)
    r = run_bass_kernel_spmd(nc, [{"in_" + n: v for n, v in arrays.items()}], core_ids=[0])
    return r.results[0]["out"].reshape(NB, T, D)
```

```python
import concourse.bass as bass
from concourse import mybir
from contextlib import ExitStack

F32 = mybir.dt.float32
I32 = mybir.dt.int32
ALU = mybir.AluOpType
ACT = mybir.ActivationFunctionType
AX = mybir.AxisListType

NB, T, D = 64, 64, 512
P = 128
DC = D // P
NP = NB // 2
NE, NA, RANK, NS = 16, 8, 16, 8
H, G, HD = 8, 4, 64
GP = G // 2
BLK, NSLOT, NBLK = 16, 257, 4112
WIN = 256
NK = WIN + T
KVD = 2 * G * HD
WSLOT = (WIN + T) // BLK + 1
NWIN = 254
RUNS = T // BLK + 1
NRUN = NB * RUNS
PREP_STEP = NP - 8
EPS = 1e-6
NONE = 60000
BIG = float(2.0 ** 100)
NEGLEN = WIN + WSLOT * BLK
BITS = 9
ROWLEN = NK + 2 ** BITS


def build(nc, a):
    ctx = ExitStack()
    with ctx:
        def sb(name, shape, dt=F32):
            return ctx.enter_context(nc.sbuf_tensor(name, shape, dt))

        def sem(name):
            return ctx.enter_context(nc.semaphore(name))

        new_rows = nc.dram_tensor("new_rows", (NB * T, KVD), F32).ap()
        x2_dram = nc.dram_tensor("x2_dram", (NP, P, D), F32).ap()
        q_dram = nc.dram_tensor("q_dram", (NB, P, GP * P), F32).ap()
        writer = nc.dram_tensor("writer", (NBLK, BLK), I32).ap()
        tok_dram = nc.dram_tensor("tok_dram", (NB, RUNS * BLK), F32).ap()
        blk_dram = nc.dram_tensor("blk_dram", (NB, RUNS), F32).ap()

        ident = sb("ident", [P, P])
        band = sb("band", [P, NK])
        neg_iota = sb("neg_iota", [P, NK])
        w1 = sb("w1", [P, DC, D])
        wqkv = sb("wqkv", [P, DC, D + KVD])
        lora_a = sb("lora_a", [P, DC, P])
        lora_b = sb("lora_b", [P, D])
        wo = sb("wo", [P, DC, D])
        gains = sb("gains", [P, 2, 4, 32])
        gain_in = sb("gain_in", [P, 2, HD])
        ids_sb = sb("ids_sb", [1, 3, NB], I32)
        lora_mask = sb("lora_mask", [P, NB])
        neg_half = sb("neg_half", [P, 12])
        thr = sb("thr", [P, NB])
        idx = sb("idx", [P, NB, 5], I32)

        scol = sb("scol", [P, 24])
        icol = sb("icol", [P, 16], I32)
        kvl_row = sb("kvl_row", [P, NB], I32)
        ad_row = sb("ad_row", [P, NB], I32)
        fcols = sb("fcols", [P, 12])
        mrow = sb("mrow", [P, RUNS * BLK])
        run_row = sb("run_row", [P, NRUN])
        win_i = sb("win_i", [P, 2, WSLOT], I32)
        win_f = sb("win_f", [P, 2, WSLOT])
        tok1 = sb("tok1", [P, RUNS * BLK])
        tmp1 = sb("tmp1", [P, RUNS * BLK])
        blk_row = sb("blk_row", [P, NRUN])
        same = sb("same", [P, 3, NRUN])
        later = sb("later", [P, NRUN])
        merged = sb("merged", [P, 3, BLK])
        merged2 = sb("merged2", [P, 3, BLK])
        merged_i = sb("merged_i", [P, 3, BLK], I32)
        run_col = sb("run_col", [P, 3])
        cnt = sb("cnt", [P, 3])
        wr_idx = sb("wr_idx", [P, 3], I32)
        table_i = sb("table_i", [P, WSLOT, BLK], I32)
        rows = [sb(f"rows{i}", [P, ROWLEN]) for i in range(2)]
        shifted = sb("shifted", [P, ROWLEN])
        bits = sb("bits", [P, BITS])
        none_i = sb("none_i", [P, NBLK * BLK // P], I32)

        ring = sb("ring", [P, 4, DC * D])
        xt = sb("xt", [P, 2, DC, P])
        x_in = sb("x_in", [P, 2, D])
        bias_in = sb("bias_in", [P, 2, D])
        cs = sb("cs", [P, 2, P])
        xb = x_in
        x1 = sb("x1", [P, 2, D])
        x1t = sb("x1t", [P, 2, DC, P])
        xam = sb("xam", [P, 2, P])
        x2 = sb("x2", [P, 2, D])
        x2t = sb("x2t", [P, 2, DC, P])
        sq = sb("sq", [P, 12, HD])
        ss = sb("ss", [P, 2, 12])
        rms = sb("rms", [P, 2, 12])
        tab = sb("tab", [P, 2, 2, 4, 32])
        rot_a = sb("rot_a", [P, 12, HD])
        rot_b = sb("rot_b", [P, 12, HD])
        rot = sb("rot", [P, 12, HD])
        q_rot = sb("q_rot", [P, 2, D])
        kv_out = sb("kv_out", [P, 2, KVD])
        q_t = sb("q_t", [P, 2, 2, DC, T])

        qpad = sb("qpad", [P, 4, G, P])
        kt = sb("kt", [P, 2, GP, NK])
        big = sb("big", [P, 2 * 2 * G * NK])
        sm = big[:, 0:2 * G * NK].rearrange("p (s g n) -> p s g n", s=2, g=G)
        prob = big[:, 2 * G * NK:].rearrange("p (s g n) -> p s g n", s=2, g=G)
        tok_row = big[:, 0:NRUN * BLK].rearrange("p (r o) -> p r o", o=BLK)
        mask = sb("mask", [P, 2, NK])
        neg_max = sb("neg_max", [P, 2, G])
        row_sum = sb("row_sum", [P, 2, G])
        recip = sb("recip", [P, 2, G])
        pt = sb("pt", [P, 2, 2, 2, P])
        pt2 = sb("pt2", [T, 2, 2, P])
        ot = sb("ot", [P, 2, DC, P])
        x2_in, x3, x4 = x_in, bias_in, x1
        bd = sb("bd", [P, 2, P])
        sbias = sb("sbias", [P, 2, 1])
        idx_now = sb("idx_now", [P, 4, 5], I32)
        kv = ring[:, :, 0:3 * KVD].rearrange("p s (c n) -> p s c n", c=3)

        ps = [ctx.enter_context(nc.psum_tensor(f"ps{i}", [P, 512], F32)) for i in range(8)]
        ps_l0, ps_t2, ps_t3, ps_t1, ps_q, ps_kv, ps_la, ps_l1 = ps
        ps_s, ps_kt, ps_pt, ps_pt2, ps_o, ps_x = ps[0:2], ps[2], ps[3:5], ps[5], ps[6], ps[7]

        ld_ids, ld_small, ld_w1, ld_wqkv, ld_late = (sem(n) for n in ("ld_ids", "ld_small", "ld_w1", "ld_wqkv", "ld_late"))
        cols_i, win_idx_ready, win_loaded = sem("cols_i"), sem("win_idx_ready"), sem("win_loaded")
        dv = sem("dv")
        pool_set, gains_ready = sem("pool_set"), sem("gains_ready")
        runs_stored, runs_loaded, none_stored = sem("runs_stored"), sem("runs_loaded"), sem("none_stored")
        merged_ready, writer_stored, table_loaded = sem("merged_ready"), sem("writer_stored"), sem("table_loaded")
        rows_ready, idx_t, idx_ready = sem("rows_ready"), sem("idx_t"), sem("idx_ready")
        ld_in = [sem(f"ld_in{i}") for i in range(2)]
        ld_w0 = [sem(f"ld_w0{i}") for i in range(4)]
        l0_done, t1_done, la_done, h_done = sem("l0_done"), sem("t1_done"), sem("la_done"), sem("h_done")
        t2_done, qkv_done, t3_done = sem("t2_done"), sem("qkv_done"), sem("t3_done")
        x1_ready, xam_ready, x2_ready = sem("x1_ready"), sem("xam_ready"), sem("x2_ready")
        ss_ready, ab_ready = sem("ss_ready"), sem("ab_ready")
        x1t_ready, x2t_ready, qt_ready, sqv_ready = sem("x1t_ready"), sem("x2t_ready"), sem("qt_ready"), sem("sqv_ready")
        xb_ready, tab_ready, rms_a, rms_ready = sem("xb_ready"), sem("tab_ready"), sem("rms_a"), sem("rms_ready")
        rot_sum, rot_ready = sem("rot_sum"), sem("rot_ready")
        st_x2 = [sem(f"st_x2{i}") for i in range(2)]
        st_kv = [sem(f"st_kv{i}") for i in range(2)]
        st_q = [sem(f"st_q{i}") for i in range(2)]
        ld_q = [sem(f"ld_q{i}") for i in range(4)]
        ld_pair = [sem(f"ld_pair{i}") for i in range(2)]
        idx_copied = sem("idx_copied")
        g_old = [sem(f"g_old{i}") for i in range(4)]
        g_new = [sem(f"g_new{i}") for i in range(4)]
        s_done, kt_done, pt_done, pv_done = sem("s_done"), sem("kt_done"), sem("pt_done"), sem("pv_done")
        wo_done, l3_done = sem("wo_done"), sem("l3_done")
        mask_ready, sm_ready, recip_ready = sem("mask_ready"), sem("sm_ready"), sem("recip_ready")
        pt_ready, pt2_ready, ot_ready = sem("pt_ready"), sem("pt2_ready"), sem("ot_ready")
        x3_ready, x4_ready = sem("x3_ready"), sem("x4_ready")
        e_ready, kt_ready, prob_ready = sem("e_ready"), sem("kt_ready"), sem("prob_ready")
        st_out = [sem(f"st_out{i}") for i in range(2)]

        SMALL_DMAS = 10
        IN_DMAS = 6
        PAIR_DMAS = 5

        def loop(eng, step, slots, first, end, last):
            for n in range(first):
                step(n, n // slots, n % slots)
            with eng.Fori(first // slots, last // slots) as j:
                for s in range(slots):
                    step(j * slots + s, j, s)
            for n in range(last, end):
                step(n, n // slots, n % slots)

        def on(n, lag, count):
            return not isinstance(n, int) or 0 <= n - lag < count

        def wait(eng, semaphore, value):
            if not isinstance(value, int) or value > 0:
                eng.wait_ge(semaphore, value)

        waits_passed = {"pool": sem("pool_waits_passed"), "dve": sem("dve_waits_passed")}

        def wait_alone(eng, name, semaphore, value):
            wait(eng, semaphore, value)
            if not isinstance(value, int):
                eng.sem_inc(waits_passed[name], 1)

        block = ctx.enter_context(nc.Block())

        @block.sync
        def _(sp):
            sp.dma_start(ids_sb[:, :, :], a["ids"]).then_inc(ld_ids, 16)
            for h in range(2):
                sp.dma_start(icol[T * h:T * h + T, 0:1], a["kvl"].rearrange("(b o) -> b o", o=1)).then_inc(ld_small, 16)
            sp.dma_start(fcols[:, :], a["fcols"]).then_inc(ld_small, 16)
            sp.dma_start(mrow[:, :], a["mrow"]).then_inc(ld_small, 16)
            sp.dma_start(run_row[:, :], a["runrow"]).then_inc(ld_small, 16)
            sp.dma_start(kvl_row[:, :], a["kvl"].partition_broadcast(P)).then_inc(ld_small, 16)
            sp.dma_start(ad_row[:, :], a["adapter"].partition_broadcast(P)).then_inc(ld_small, 16)
            sp.dma_start(scol[:, 0:1], a["scal"]).then_inc(ld_small, 16)
            sp.dma_start(gain_in[:, 0, :], a["qn"].partition_broadcast(P)).then_inc(ld_small, 16)
            sp.dma_start(gain_in[:, 1, :], a["kn"].partition_broadcast(P)).then_inc(ld_small, 16)
            sp.wait_ge(ld_ids, 16)

            def load_in(k, j, s):
                wait(sp, l0_done, k - 1)
                wait(sp, x1_ready, k - 1)
                wait(sp, tab_ready, k - 1)
                sp.dma_start(xt[:, s, :, :], a["xt"][bass.ds(k, 1)].rearrange("o p c t -> (o p) c t")).then_inc(ld_in[s], 16)
                sp.dma_start(x_in[:, s, :], a["x"][bass.ds(k, 1)].rearrange("o p d -> (o p) d")).then_inc(ld_in[s], 16)
                for h in range(2):
                    e = sp.value_load(ids_sb[0:1, 0, bass.ds(k * 2 + h, 1)], min_val=0, max_val=NE - 1)
                    sp.dma_start(ring[:, 2 * s + h, :], a["w0"][bass.ds(e, 1)].rearrange("o p n -> (o p) n")).then_inc(
                        ld_w0[2 * s + h], 16)
                    sp.dma_start(bias_in[T * h:T * h + T, s, :], a["b0"][bass.ds(e, 1)].rearrange(
                        "o d -> (o d)").partition_broadcast(T)).then_inc(ld_in[s], 16)
                    p0 = sp.value_load(ids_sb[0:1, 2, bass.ds(k * 2 + h, 1)], min_val=0, max_val=NSLOT * BLK - T)
                    sp.dma_start(cs[T * h:T * h + T, s, :], a["rope"][bass.ds(p0, T), :]).then_inc(ld_in[s], 16)

            load_in(0, 0, 0)
            sp.dma_start(ident[:, :], a["ident"]).then_inc(ld_w1, 16)
            sp.dma_start(lora_a[:, :, :], a["la"]).then_inc(ld_w1, 16)
            sp.dma_start(w1[:, :, :], a["w1"]).then_inc(ld_w1, 16)
            sp.dma_start(lora_b[:, :], a["lb"]).then_inc(ld_w1, 16)
            load_in(1, 0, 1)
            sp.dma_start(wqkv[:, :, 0:D], a["wq"]).then_inc(ld_wqkv, 16)
            sp.dma_start(wqkv[:, :, D:D + 256], a["wk"]).then_inc(ld_wqkv, 16)
            sp.dma_start(wqkv[:, :, D + 256:], a["wv"]).then_inc(ld_wqkv, 16)

            def phase_one(k, j, s):
                if on(k, 0, NP):
                    load_in(k, j, s)
                if on(k, 3, NP):
                    t = (s + 1) % 2
                    sp.wait_ge(x2_ready, k - 2)
                    sp.dma_start(x2_dram[bass.ds(k - 3, 1)].rearrange("o p d -> (o p) d"), x2[:, t, :]).then_inc(st_x2[t], 16)
                if on(k, 4, NP):
                    sp.wait_ge(rot_ready, k - 3)
                    sp.wait_ge(sqv_ready, k - 3)
                    sp.dma_start(new_rows[bass.ds((k - 4) * P, P), :], kv_out[:, s, :]).then_inc(st_kv[s], 16)

            for k in range(2, 4):
                phase_one(k, k // 2, k % 2)
            sp.dma_start(wo[:, :, :], a["wo"]).then_inc(ld_late, 16)
            sp.dma_start(band[:, :], a["band"]).then_inc(ld_late, 16)
            sp.dma_start(neg_iota[:, :], a["negiota"]).then_inc(ld_late, 16)
            sp.wait_ge(pool_set, 1)
            sp.dma_start(writer.rearrange("n o -> (n o)").rearrange("(p m) -> p m", p=P), none_i[:, :]).then_inc(none_stored, 16)
            sp.wait_ge(cols_i, 1)
            sp.dma_start(tok_dram, tok1[0:NB, :]).then_inc(runs_stored, 16)
            sp.dma_start(blk_dram, win_f[0:NB, 1, 0:RUNS]).then_inc(runs_stored, 16)
            sp.wait_ge(runs_stored, 32)
            sp.dma_start(tok_row.rearrange("p r o -> p (r o)"), tok_dram.rearrange("b n -> (b n)").partition_broadcast(P)).then_inc(
                runs_loaded, 16)
            sp.dma_start(blk_row[:, :], blk_dram.rearrange("b n -> (b n)").partition_broadcast(P)).then_inc(runs_loaded, 16)
            with sp.Fori(2, NP // 2) as j:
                for s in range(2):
                    phase_one(j * 2 + s, j, s)
            for k in range(NP, NP + 4):
                phase_one(k, k // 2, k % 2)

            for s in range(2):
                sp.wait_ge(st_q[s], NP // 2 * 16)
                sp.wait_ge(st_x2[s], NP // 2 * 16)
            sp.wait_ge(pool_set, 3)

            def load_queries(b, s):
                wait(sp, s_done, b * G - 3 * G if not isinstance(b, int) or b >= 4 else 0)
                src = q_dram[bass.ds(b, 1)].rearrange("o p (g m) -> (o p) g m", g=GP)
                for q in range(2):
                    dst = qpad[HD * q:HD * q + HD, s, :, :].rearrange("p (g q) m -> p g q m", q=2)[:, :, q, :]
                    sp.dma_start(dst, src[HD * q:HD * q + HD]).then_inc(ld_q[s], 16)

            for b in range(2):
                load_queries(b, b)

            def phase_two(b, j, s):
                if on(b, -2, NB):
                    load_queries(b + 2, (s + 2) % 4)
                if s % 2 == 0 and on(b, 6, NB):
                    k, t = (b // 2 if isinstance(b, int) else j * 2 + s // 2) - 3, 1 - s // 2
                    sp.wait_ge(x4_ready, k + 1)
                    sp.dma_start(a["out"][bass.ds(k, 1)].rearrange("o p d -> (o p) d"), x4[:, t, :]).then_inc(st_out[t], 16)
                if s % 2 == 0 and on(b, 2, NB):
                    k, t = (b // 2 if isinstance(b, int) else j * 2 + s // 2) - 1, 1 - s // 2
                    wait(sp, x4_ready, k - 1)
                    sp.dma_start(x2_in[:, t, :], x2_dram[bass.ds(k, 1)].rearrange("o p d -> (o p) d")).then_inc(ld_pair[t], 16)
                    for h in range(2):
                        u = sp.value_load(ids_sb[0:1, 1, bass.ds(k * 2 + h, 1)], min_val=0, max_val=NS - 1)
                        sp.dma_start(bd[T * h:T * h + T, t, T * h:T * h + T],
                                     a["w3"][bass.ds(u, 1)].rearrange("o c d -> (o c) d")).then_inc(ld_pair[t], 16)
                        sp.dma_start(sbias[T * h:T * h + T, t, :],
                                     a["b3"][bass.ds(u, 1)].rearrange("o d n -> (o d) n")).then_inc(ld_pair[t], 16)

            loop(sp, phase_two, 4, 8, NB + 6, NB - 4)
            for t in range(2):
                sp.wait_ge(st_out[t], NP // 2 * 16)
                sp.wait_ge(st_kv[t], NP // 2 * 16)
            sp.wait_ge(writer_stored, 48)
            sp.wait_ge(none_stored, 16)

        @block.gpsimd
        def _(pool):
            nc.gpsimd.memset(none_i[:, :], NONE).then_inc(pool_set, 1)
            nc.gpsimd.memset(neg_half[:, :], -0.5).then_inc(pool_set, 1)
            nc.gpsimd.memset(bd[:, :, :], 0.0)
            nc.gpsimd.memset(qpad[:, :, :, :], 0.0).then_inc(pool_set, 1)
            pool.wait_ge(win_idx_ready, 1)
            for w in range(2):
                pool.indirect_dma_start(out=win_i[:, w, :], out_offset=None, in_=a["windows"],
                                        in_offset=bass.IndirectOffsetOnAxis(ap=icol[:, 4 + w:5 + w], axis=0)).then_inc(win_loaded, 16)

            def store_writers():
                pool.wait_ge(none_stored, 16)
                pool.wait_ge(merged_ready, 1)
                for m in range(3):
                    n = P if m < 2 else NB
                    pool.indirect_dma_start(out=writer, out_offset=bass.IndirectOffsetOnAxis(ap=wr_idx[0:n, m:m + 1], axis=0),
                                            in_=merged_i[0:n, m, :], in_offset=None,
                                            bounds_check=NBLK - 1, oob_is_err=False).then_inc(writer_stored, 16)

            def load_writers(w0, w1):
                pool.wait_ge(writer_stored, 48)
                for w in range(w0, w1):
                    pool.indirect_dma_start(out=table_i[:, w, :], out_offset=None, in_=writer,
                                            in_offset=bass.IndirectOffsetOnAxis(ap=win_i[:, 0, w:w + 1], axis=0)).then_inc(
                                                table_loaded, 16)

            def sum_x_bias(k, j, s):
                pool.wait_ge(ld_in[s], IN_DMAS * 16 * (j + 1))
                nc.gpsimd.tensor_tensor(xb[:, s, :], x_in[:, s, :], bias_in[:, s, :], ALU.add).then_inc(xb_ready, 1)

            SIDE = {PREP_STEP + 3: store_writers}
            for n in range(3):
                SIDE[PREP_STEP + 4 + n] = lambda n=n: load_writers(7 * n, 7 * n + 7)

            def phase_one(k, j, s):
                if on(k, 2, NP):
                    pool.wait_ge(ss_ready, k - 1)
                    nc.gpsimd.tensor_tensor(rms[:, s, :], ss[:, s, :], neg_half[:, :], ALU.pow).then_inc(rms_ready, 1)
                    pool.wait_ge(ab_ready, k - 1)
                    wait(pool, rot_ready, k - 2)
                    nc.gpsimd.tensor_tensor(rot[:, :, :], rot_a[:, :, :], rot_b[:, :, :], ALU.add).then_inc(rot_sum, 1)
                    pool.wait_ge(rot_sum, k - 1)
                    pool.wait_ge(rms_ready, k - 1)
                    wait(pool, t3_done, k - 3)
                    wait(pool, st_kv[s], 16 * (j - 1))
                    nc.gpsimd.tensor_tensor(q_rot[:, s, :].rearrange("p (g d) -> p g d", d=HD), rot[:, 0:8, :],
                                            rms[:, s, 0:8].unsqueeze(2).to_broadcast([P, 8, HD]), ALU.mult)
                    nc.gpsimd.tensor_tensor(kv_out[:, s, 0:256].rearrange("p (g d) -> p g d", d=HD), rot[:, 8:12, :],
                                            rms[:, s, 8:12].unsqueeze(2).to_broadcast([P, 4, HD]), ALU.mult).then_inc(rot_ready, 1)
                if on(k, -1, NP):
                    sum_x_bias(k + 1, j + s, 1 - s)
                if on(k, 0, NP):
                    wait(pool, ab_ready, k - 1)
                    nc.gpsimd.tensor_tensor(tab[:, s, :, :, :].rearrange("p w f n -> p w (f n)"),
                                            gains[:, :, :, :].rearrange("p w f n -> p w (f n)"),
                                            cs[:, s, :].unsqueeze(1).to_broadcast([P, 2, P]), ALU.mult).then_inc(tab_ready, 1)
                if isinstance(k, int) and k in SIDE:
                    SIDE[k]()

            sum_x_bias(0, 0, 0)
            pool.wait_ge(gains_ready, 1)
            loop(pool, phase_one, 2, 4, NP + 2, PREP_STEP)

            pool.wait_ge(idx_ready, 1)
            pool.wait_ge(l0_done, NP)

            def gather_old(b, j, s):
                wait_alone(pool, "pool", pv_done, 2 * b - 6 if not isinstance(b, int) or b >= 4 else 0)
                nc.gpsimd.tensor_copy(idx_now[:, s, :], idx[:, bass.ds(b, 1), :].rearrange("p o n -> p (o n)")).then_inc(idx_copied, 1)
                wait_alone(pool, "pool", idx_copied, b + 1)
                for c in range(2):
                    pool.indirect_dma_start(out=kv[:, s, c, :], out_offset=None, in_=a["kvrows"],
                                            in_offset=bass.IndirectOffsetOnAxis(ap=idx_now[:, s, c:c + 1], axis=0)).then_inc(g_old[s], 16)

            def gather_new(b, j, s):
                pool.indirect_dma_start(out=kv[0:T, s, 2, :], out_offset=None, in_=new_rows,
                                        in_offset=bass.IndirectOffsetOnAxis(ap=idx_now[0:T, s, 4:5], axis=0)).then_inc(g_new[s], 16)
                wait_alone(pool, "pool", g_old[s], 32 * (j + 1))
                for c in range(2):
                    pool.indirect_dma_start(out=kv[:, s, c, :], out_offset=None, in_=new_rows,
                                            in_offset=bass.IndirectOffsetOnAxis(ap=idx_now[:, s, 2 + c:3 + c], axis=0),
                                            bounds_check=NB * T - 1, oob_is_err=False).then_inc(g_new[s], 16)

            gather_old(0, 0, 0)
            gather_old(1, 0, 1)
            for s in range(2):
                pool.wait_ge(st_kv[s], NP // 2 * 16)
            gather_new(0, 0, 0)
            gather_new(1, 0, 1)

            def phase_two(b, j, s):
                gather_old(b, j, s)
                gather_new(b, j, s)

            for b in range(2, 4):
                phase_two(b, 0, b)
            with pool.Fori(1, NB // 4) as j:
                for s in range(4):
                    phase_two(j * 4 + s, j, s)

        @block.tensor
        def _(pe):
            def phase_one(k, j, s):
                r = 1 - s
                if on(k, 0, NP):
                    pe.wait_ge(ld_in[s], IN_DMAS * 16 * (j + 1))
                    pe.wait_ge(ld_w0[2 * s], 16 * (j + 1))
                    pe.wait_ge(ld_w0[2 * s + 1], 16 * (j + 1))
                    wait(pe, x1_ready, k)
                    for c in range(DC):
                        for h in range(2):
                            last = nc.tensor.matmul(ps_l0[T * h:T * h + T, :], xt[:, s, c, T * h:T * h + T],
                                                    ring[:, 2 * s + h, c * D:(c + 1) * D], start=(c == 0), stop=(c == DC - 1))
                    last.then_inc(l0_done, 1)
                if on(k, 1, NP):
                    pe.wait_ge(x2_ready, k)
                    wait(pe, x2t_ready, k - 1)
                    for c in range(DC):
                        last = nc.tensor.transpose(ps_t2[:, c * P:(c + 1) * P], x2[:, r, c * P:(c + 1) * P], ident[:, :])
                    last.then_inc(t2_done, 1)
                if isinstance(k, int) and k == NP:
                    pe.wait_ge(rows_ready, 1)
                    pe.wait_ge(x1t_ready, NP)
                    for c in range(3):
                        n = P if c < 2 else T
                        last = nc.tensor.transpose(ps_t1[0:n, c * P:(c + 1) * P], rows[1][:, c * P:c * P + n], ident[:, :])
                    last.then_inc(idx_t, 1)
                if on(k, 2, NP):
                    pe.wait_ge(rot_ready, k - 1)
                    wait(pe, qt_ready, k - 2)
                    for c in range(DC):
                        last = nc.tensor.transpose(ps_t3[:, c * P:(c + 1) * P], q_rot[:, s, c * P:(c + 1) * P], ident[:, :])
                    last.then_inc(t3_done, 1)
                if on(k, 0, NP):
                    pe.wait_ge(x1_ready, k + 1)
                    wait(pe, x1t_ready, k)
                    if isinstance(k, int) and k == 0:
                        pe.wait_ge(ld_w1, 4 * 16)
                    for c in range(DC):
                        last = nc.tensor.transpose(ps_t1[:, c * P:(c + 1) * P], x1[:, s, c * P:(c + 1) * P], ident[:, :])
                    last.then_inc(t1_done, 1)
                if on(k, 1, NP):
                    pe.wait_ge(x2t_ready, k)
                    if isinstance(k, int) and k == 1:
                        pe.wait_ge(ld_wqkv, 3 * 16)
                    wait(pe, ab_ready, k - 1)
                    wait(pe, sqv_ready, k - 1)
                    for c in range(DC):
                        nc.tensor.matmul(ps_q[:, :], x2t[:, r, c, :], wqkv[:, c, 0:D], start=(c == 0), stop=(c == DC - 1))
                    for c in range(DC):
                        last = nc.tensor.matmul(ps_kv[:, :], x2t[:, r, c, :], wqkv[:, c, D:D + KVD], start=(c == 0), stop=(c == DC - 1))
                    last.then_inc(qkv_done, 1)
                if on(k, 0, NP):
                    pe.wait_ge(x1t_ready, k + 1)
                    wait(pe, xam_ready, k)
                    for c in range(DC):
                        last = nc.tensor.matmul(ps_la[:, 0:P], lora_a[:, c, :], x1t[:, s, c, :], start=(c == 0), stop=(c == DC - 1))
                    last.then_inc(la_done, 1)
                    wait(pe, x2_ready, k)
                    for c in range(DC):
                        nc.tensor.matmul(ps_l1[:, :], x1t[:, s, c, :], w1[:, c, :], start=(c == 0), stop=False)
                    pe.wait_ge(xam_ready, k + 1)
                    nc.tensor.matmul(ps_l1[:, :], xam[:, s, :], lora_b[:, :], start=False, stop=True).then_inc(h_done, 1)

            loop(pe, phase_one, 2, 4, NP + 2, NP)

            pe.wait_ge(idx_ready, 1)
            pe.wait_ge(x2_ready, NP)
            pe.wait_ge(ab_ready, NP)
            pe.wait_ge(sqv_ready, NP)
            pe.wait_ge(qt_ready, NP)
            pe.wait_ge(ld_late, 3 * 16)

            def transpose_keys(b, j, s, p):
                if p == 0:
                    pe.wait_ge(g_old[s], 32 * (j + 1))
                    pe.wait_ge(g_new[s], 48 * (j + 1))
                wait(pe, kt_ready, 2 * b + p)
                for c in range(3):
                    n = P if c < 2 else T
                    last = nc.tensor.transpose(ps_kt[:, c * P:c * P + n], kv[0:n, s, c, p * P:(p + 1) * P], ident[0:n, 0:n])
                last.then_inc(kt_done, 1)

            for p in range(GP):
                transpose_keys(0, 0, 0, p)

            def phase_two(b, j, s):
                r = (s - 1) % 4
                first_half, second_half = s % 2 == 1 and on(b, 3, NB), s % 2 == 0 and on(b, 4, NB)
                pair = (b // 2 if isinstance(b, int) else j * 2 + s // 2) - (1 if s % 2 else 2)
                pair_s = (s // 2 + s % 2) % 2

                def scores(g):
                    wait(pe, sm_ready, G * b + g - 1)
                    if g % 2 == 0:
                        pe.wait_ge(kt_ready, 2 * b + g // 2 + 1)
                    if g == 0:
                        pe.wait_ge(ld_q[s], 32 * (j + 1))
                    nc.tensor.matmul(ps_s[g % 2][:, 0:NK], qpad[:, s, g, :], kt[:, s % 2, g // 2, :],
                                     start=True, stop=True).then_inc(s_done, 1)

                def transpose_probs(p):
                    pe.wait_ge(prob_ready, G * b - G + 2 * p + 2)
                    wait(pe, pt_ready, 2 * b - 3 + p)
                    wait(pe, pt2_ready, 2 * b - 2 + p)
                    for q in range(2):
                        for c in range(3):
                            n = P if c < 2 else T
                            dst = ps_pt[p][:, (q * 2 + c) * P:(q * 2 + c + 1) * P] if c < 2 else \
                                ps_pt2[0:T, (p * 2 + q) * P:(p * 2 + q + 1) * P]
                            last = nc.tensor.transpose(dst, prob[:, r % 2, 2 * p + q, c * P:c * P + n], ident[:, :])
                    last.then_inc(pt_done, 1)

                def values(p):
                    pe.wait_ge(pt_ready, 2 * b - 1 + p)
                    pe.wait_ge(pt2_ready, 2 * b - 1 + p)
                    if p == 0:
                        wait(pe, ot_ready, b - 1)
                    for c in range(3):
                        n = P if c < 2 else T
                        for q in range(2):
                            rhs = pt[:, p, q, c, :] if c < 2 else pt2[:, p, q, :]
                            v0 = G * HD + (2 * p + q) * HD
                            last = nc.tensor.matmul(ps_o[HD * q:HD * q + HD, p * P:(p + 1) * P], kv[0:n, r, c, v0:v0 + HD], rhs,
                                                    start=(c == 0), stop=(c == 2))
                    last.then_inc(pv_done, 1)

                def project(chunks):
                    for c in chunks:
                        last = nc.tensor.matmul(ps_x[:, :], ot[:, pair_s, c, :], wo[:, c, :], start=(c == 0), stop=(c == DC - 1))
                    return last

                if on(b, 0, NB):
                    scores(0)
                    scores(1)
                if on(b, 1, NB):
                    transpose_probs(0)
                if on(b, 0, NB):
                    scores(2)
                    scores(3)
                if on(b, -1, NB):
                    transpose_keys(b + 1, j + (s == 3), (s + 1) % 4, 0)
                if on(b, 1, NB):
                    transpose_probs(1)
                if first_half:
                    pe.wait_ge(ot_ready, 2 * pair + 2)
                    wait(pe, x4_ready, pair)
                    project(range(DC // 2))
                if second_half:
                    project(range(DC // 2, DC)).then_inc(wo_done, 1)
                if on(b, 1, NB):
                    values(0)
                if on(b, -1, NB):
                    transpose_keys(b + 1, j + (s == 3), (s + 1) % 4, 1)
                if second_half:
                    pe.wait_ge(x3_ready, pair + 1)
                    pe.wait_ge(ld_pair[pair_s], PAIR_DMAS * 16 * j)
                    nc.tensor.matmul(ps_x[:, :], bd[:, pair_s, :], x3[:, pair_s, :], start=True, stop=True).then_inc(l3_done, 1)
                if on(b, 1, NB):
                    values(1)

            loop(pe, phase_two, 4, 4, NB + 3, NB - 4)

        @block.scalar
        def _(act):
            def phase_one(k, j, s):
                r = 1 - s
                if on(k, 1, NP):
                    act.wait_ge(t2_done, k)
                    wait(act, qkv_done, k - 2)
                    nc.scalar.activation(x2t[:, r, :, :].rearrange("p c t -> p (c t)"), ps_t2[:, :], ACT.Copy).then_inc(x2t_ready, 1)
                if on(k, 2, NP):
                    act.wait_ge(t3_done, k - 1)
                    wait(act, st_q[s], 16 * j - 16)
                    nc.scalar.activation(q_t[:, s, :, :, :], ps_t3[:, :].rearrange("p (c h t) -> p h c t", c=DC, h=2),
                                         ACT.Copy).then_inc(qt_ready, 1)
                if on(k, 0, NP):
                    act.wait_ge(t1_done, k + 1)
                    wait(act, h_done, k - 1)
                    nc.scalar.activation(x1t[:, s, :, :].rearrange("p c t -> p (c t)"), ps_t1[:, :], ACT.Copy).then_inc(x1t_ready, 1)
                if on(k, 2, NP):
                    act.wait_ge(qt_ready, k - 1)
                    act.dma_start(q_dram[bass.ds(k * 2 - 4, 2)].rearrange("h p n -> p h n"),
                                  q_t[:, s, :, :, :].rearrange("p h c t -> p h (c t)")).then_inc(st_q[s], 16)
                if on(k, 1, NP):
                    act.wait_ge(qkv_done, k)
                    wait(act, ss_ready, k - 1)
                    nc.scalar.activation(sq[:, 0:8, :].rearrange("p g d -> p (g d)"), ps_q[:, :], ACT.Square)
                    nc.scalar.activation(sq[:, 8:12, :].rearrange("p g d -> p (g d)"), ps_kv[:, 0:256], ACT.Square)
                    wait(act, st_kv[r], 16 * (j - 1 + s))
                    nc.scalar.activation(kv_out[:, r, 256:512], ps_kv[:, 256:512], ACT.Copy).then_inc(sqv_ready, 1)

            loop(act, phase_one, 2, 4, NP + 2, NP)

            def copy_keys(b, s, p):
                act.wait_ge(kt_done, 2 * b + p + 1)
                wait(act, s_done, G * b - G if not isinstance(b, int) or b >= 2 else 0)
                nc.scalar.activation(kt[:, s % 2, p, :], ps_kt[:, 0:NK], ACT.Copy).then_inc(kt_ready, 1)

            for p in range(GP):
                copy_keys(0, 0, p)

            def phase_two(b, j, s):
                def exps(g):
                    act.wait_ge(sm_ready, G * b + g + 1)
                    wait(act, pt_done, 2 * b - 2)
                    nc.scalar.activation(prob[:, s % 2, g, :], sm[:, s % 2, g, :], ACT.Exp, bias=neg_max[:, s % 2, g:g + 1],
                                         scale=-1.0, accum_out=row_sum[:, s % 2, g:g + 1]).then_inc(e_ready, 1)

                def copy_own(p):
                    act.wait_ge(pt_done, 2 * b - 1 + p)
                    wait(act, pv_done, 2 * b - 3 + p)
                    nc.scalar.activation(pt2[:, p, :, :].rearrange("p q t -> p (q t)"),
                                         ps_pt2[0:T, p * 2 * P:(p + 1) * 2 * P], ACT.Copy).then_inc(pt2_ready, 1)

                if on(b, 0, NB):
                    exps(0)
                    exps(1)
                if on(b, 1, NB):
                    copy_own(0)
                if on(b, 0, NB):
                    exps(2)
                if on(b, 1, NB):
                    copy_own(1)
                if on(b, 0, NB):
                    exps(3)
                if on(b, -1, NB):
                    copy_keys(b + 1, s + 1, 0)
                    copy_keys(b + 1, s + 1, 1)

            loop(act, phase_two, 4, 4, NB + 1, NB - 4)

        @block.vector
        def _(dve):
            chain = [0]

            def link(ins):
                chain[0] += 1
                ins.then_inc(dv, 1)
                dve.wait_ge(dv, chain[0])

            V = nc.vector
            BCOL, ACOL, BROW, R0 = 0, 1, 2, 3
            dve.wait_ge(ld_small, SMALL_DMAS * 16)
            link(V.tensor_scalar(icol[:, 1:2], icol[:, 0:1], BLK - 1, None, ALU.bitwise_and))
            link(V.tensor_scalar(icol[:, 2:3], icol[:, 0:1], float(WIN), 0.0, ALU.subtract, ALU.max))
            link(V.tensor_scalar(icol[:, 3:4], icol[:, 2:3], 4, None, ALU.logical_shift_right))
            link(V.tensor_scalar(icol[:, 6:7], icol[:, 0:1], 4, None, ALU.logical_shift_right))
            link(V.tensor_tensor(icol[:, 4:5], icol[:, 3:4], fcols[:, BROW:BROW + 1], ALU.add))
            V.tensor_tensor(icol[:, 5:6], icol[:, 6:7], fcols[:, BROW:BROW + 1], ALU.add).then_inc(win_idx_ready, 1)
            link(V.tensor_scalar(scol[:, 1:2], icol[:, 0:1], float(WIN), None, ALU.is_ge))
            link(V.tensor_tensor(scol[:, 2:3], scol[:, 1:2], icol[:, 1:2], ALU.mult))
            link(V.scalar_tensor_tensor(icol[:, 7:8], icol[:, 0:1], float(WIN), scol[:, 2:3], ALU.min, ALU.add))
            for n in range(BITS):
                link(V.tensor_scalar(icol[:, 8:9], icol[:, 7:8], n, 1, ALU.logical_shift_right, ALU.bitwise_and))
                link(V.tensor_copy(bits[:, n:n + 1], icol[:, 8:9]))
            link(V.tensor_copy(scol[:, 3:4], icol[:, 1:2]))
            link(V.tensor_scalar(tmp1[:, :], mrow[:, :], scol[:, 3:4], None, ALU.subtract))
            link(V.tensor_scalar(tok1[:, :], tmp1[:, :], fcols[:, BCOL:BCOL + 1], None, ALU.add))
            link(V.scalar_tensor_tensor(tok1[:, :], tmp1[:, :], 0.0, tok1[:, :], ALU.is_ge, ALU.mult))
            link(V.scalar_tensor_tensor(tok1[:, :], tmp1[:, :], float(T - 1), tok1[:, :], ALU.is_le, ALU.mult))
            link(V.tensor_scalar(lora_mask[:, :], ad_row[:, :], fcols[:, ACOL:ACOL + 1], scol[:, 0:1], ALU.is_equal, ALU.mult))
            link(V.tensor_scalar(thr[:, :], kvl_row[:, :], -BIG, BIG * WIN, ALU.mult, ALU.add))
            link(V.tensor_scalar(gain_in[:, :, :], gain_in[:, :, :], 1.0, None, ALU.add))
            for w, g in ((0, -1.0 / 16.0), (1, 1.0)):
                for f, half, sign in ((0, 0, 1.0), (1, 1, 1.0), (2, 1, -1.0), (3, 0, 1.0)):
                    link(V.tensor_scalar(gains[:, w, f, :], gain_in[:, w, 32 * half:32 * half + 32], g * sign, None, ALU.mult))
            V.tensor_copy(scol[:, 4:5], scol[:, 3:4]).then_inc(gains_ready, 1)

            def take_tables():
                dve.wait_ge(win_loaded, 32)
                link(V.tensor_copy(win_f[:, :, :], win_i[:, :, :]))
                V.tensor_copy(scol[:, 5:6], scol[:, 3:4]).then_inc(cols_i, 1)
                for m in range(3):
                    for h in range(2 if m < 2 else 1):
                        link(V.tensor_copy(run_col[T * h:T * h + T, m:m + 1], win_f[T * h:T * h + T, 1, 2 * m + h:2 * m + h + 1]))

            def merge_runs(m):
                dve.wait_ge(runs_loaded, 32)
                n = P if m < 2 else NB
                link(V.tensor_scalar(same[0:n, m, :], blk_row[0:n, :], run_col[0:n, m:m + 1], None, ALU.is_equal))
                link(V.scalar_tensor_tensor(later[0:n, :], run_row[0:n, :], fcols[0:n, R0 + m:R0 + m + 1], same[0:n, m, :],
                                            ALU.is_gt, ALU.mult, accum_out=cnt[0:n, m:m + 1]))
                for o in range(BLK):
                    link(V.tensor_tensor_reduce(later[0:n, :], same[0:n, m, :], tok_row[0:n, :, o], 1.0, 0.0, ALU.mult, ALU.max,
                                                accum_out=merged[0:n, m, o:o + 1]))
                link(V.scalar_tensor_tensor(wr_idx[0:n, m:m + 1], cnt[0:n, m:m + 1], 8192.0, run_col[0:n, m:m + 1], ALU.mult, ALU.add))
                link(V.tensor_scalar(merged2[0:n, m, :], merged[0:n, m, :], 0.0, NONE + 1.0, ALU.is_equal, ALU.mult))
                link(V.scalar_tensor_tensor(merged_i[0:n, m, :], merged[0:n, m, :], -1.0, merged2[0:n, m, :], ALU.add, ALU.add))
                if m == 2:
                    V.tensor_copy(scol[:, 6:7], scol[:, 3:4]).then_inc(merged_ready, 1)

            def make_rows():
                link(V.memset(rows[0][:, NEGLEN:], 0.0))
                link(V.tensor_scalar(win_f[:, 0, :], win_f[:, 0, :], float(BLK), None, ALU.mult))
                link(V.tensor_tensor(rows[0][0:NB, WIN:NEGLEN].rearrange("p (w o) -> p w o", o=BLK),
                                     win_f[0:NB, 0, :].unsqueeze(2).to_broadcast([NB, WSLOT, BLK]),
                                     mrow[0:NB, 0:BLK].unsqueeze(1).to_broadcast([NB, WSLOT, BLK]), ALU.add))
                dve.wait_ge(table_loaded, 16 * WSLOT)
                link(V.tensor_copy(rows[0][NB:P, WIN:NEGLEN], table_i[NB:P, :, :].rearrange("p w o -> p (w o)")))
                link(V.tensor_copy(rows[0][:, 0:WIN], rows[0][:, WIN:WIN + 1].to_broadcast([P, WIN])))
                for i, n in enumerate(reversed(range(BITS))):
                    size = NK + 2 ** n - 1
                    src, dst = rows[i % 2], rows[(i + 1) % 2]
                    link(V.tensor_tensor(shifted[:, 0:size], src[:, 2 ** n:2 ** n + size], src[:, 0:size], ALU.subtract))
                    link(V.scalar_tensor_tensor(dst[:, 0:size], shifted[:, 0:size], bits[:, n:n + 1], src[:, 0:size], ALU.mult, ALU.add))
                V.tensor_copy(scol[:, 7:8], scol[:, 3:4]).then_inc(rows_ready, 1)

            def take_indices():
                dve.wait_ge(idx_t, 1)
                tview = ps_t1[:, :].rearrange("p (c w b) -> p c w b", c=4, w=2)
                for c, w, col in ((0, 0, 0), (1, 0, 1), (0, 1, 2), (1, 1, 3)):
                    V.tensor_copy(idx[:, :, col], tview[:, c, w, :])
                V.memset(idx[T:P, :, 4], 0)
                V.tensor_copy(idx[0:T, :, 4], tview[0:T, 2, 1, :]).then_inc(idx_ready, 1)

            SIDE = {2: take_tables, NP - 1: make_rows, NP: take_indices}
            for m in range(3):
                SIDE[PREP_STEP + m] = lambda m=m: merge_runs(m)

            def phase_one(k, j, s):
                r = 1 - s
                if on(k, 0, NP):
                    dve.wait_ge(l0_done, k + 1)
                    dve.wait_ge(xb_ready, k + 1)
                    wait(dve, t1_done, k - 1)
                    wait(dve, x2_ready, k - 1)
                    V.tensor_tensor(x1[:, s, :], ps_l0[:, :], xb[:, s, :], ALU.add).then_inc(x1_ready, 1)
                if isinstance(k, int) and k in SIDE:
                    SIDE[k]()
                if on(k, 0, NP):
                    dve.wait_ge(la_done, k + 1)
                    wait(dve, h_done, k - 1)
                    V.tensor_tensor(xam[:, s, :].rearrange("p (h t) -> p h t", h=2), ps_la[:, 0:P].rearrange("p (h t) -> p h t", h=2),
                                    lora_mask[:, bass.ds(k * 2, 2)].unsqueeze(2).to_broadcast([P, 2, T]), ALU.mult).then_inc(xam_ready, 1)
                if on(k, 1, NP):
                    dve.wait_ge(sqv_ready, k)
                    wait(dve, rms_ready, k - 2)
                    V.tensor_reduce(ss[:, r, :], sq[:, :, :], AX.X, ALU.add).then_inc(rms_a, 1)
                    dve.wait_ge(rms_a, k)
                    V.tensor_scalar(ss[:, r, :], ss[:, r, :], 1.0 / HD, EPS, ALU.mult, ALU.add).then_inc(ss_ready, 1)
                    dve.wait_ge(tab_ready, k)
                    wait(dve, rot_sum, k - 1)
                    for w, src, g0, n in ((0, ps_q, 0, 8), (1, ps_kv, 8, 4)):
                        u = src[:, 0:n * HD].rearrange("p (g d) -> p g d", d=HD)
                        t = tab[:, r, w, :, :]
                        V.tensor_tensor(rot_a[:, g0:g0 + n, :], u, t[:, 0:2, :].rearrange("p f n -> p (f n)").unsqueeze(1).to_broadcast(
                            [P, n, HD]), ALU.mult)
                        V.tensor_tensor(rot_b[:, g0:g0 + n, 0:32], u[:, :, 32:64], t[:, 2, :].unsqueeze(1).to_broadcast([P, n, 32]), ALU.mult)
                        last = V.tensor_tensor(rot_b[:, g0:g0 + n, 32:64], u[:, :, 0:32], t[:, 3, :].unsqueeze(1).to_broadcast([P, n, 32]),
                                               ALU.mult)
                    last.then_inc(ab_ready, 1)
                if on(k, 0, NP):
                    dve.wait_ge(h_done, k + 1)
                    wait(dve, t2_done, k - 1)
                    wait(dve, st_x2[s], 16 * j)
                    V.tensor_tensor(x2[:, s, :], ps_l1[:, :], x1[:, s, :], ALU.add).then_inc(x2_ready, 1)

            loop(dve, phase_one, 2, 4, NP + 2, PREP_STEP)

            def make_mask(b, s):
                wait(dve, sm_ready, G * b - G)
                V.scalar_tensor_tensor(mask[:, s % 2, :], neg_iota[:, :], thr[:, bass.ds(b, 1)], band[:, :],
                                       ALU.add, ALU.max).then_inc(mask_ready, 1)

            dve.wait_ge(ld_late, 3 * 16)
            make_mask(0, 0)

            def phase_two(b, j, s):
                def copy_probs(p):
                    dve.wait_ge(pt_done, 2 * b - 1 + p)
                    wait(dve, pv_done, 2 * b - 3 + p)
                    V.tensor_copy(pt[:, p, :, :, :].rearrange("p q c t -> p (q c t)"), ps_pt[p][:, :]).then_inc(pt_ready, 1)

                def copy_outputs():
                    pair = (b - 1) // 2 if isinstance(b, int) else j * 2 + (s - 1) // 2
                    dve.wait_ge(pv_done, 2 * b)
                    wait(dve, wo_done, pair - 1)
                    h = (s - 1) % 2
                    V.tensor_copy(ot[:, ((s - 1) % 4) // 2, :, T * h:T * h + T],
                                  ps_o[:, 0:2 * P].rearrange("p (c t) -> p c t", c=2 * GP)).then_inc(ot_ready, 1)

                turn = s % 2 == 0 and on(b, 4, NB)
                pair, pair_s = (b // 2 if isinstance(b, int) else j * 2 + s // 2) - 2, s // 2

                def masked(g):
                    dve.wait_ge(s_done, G * b + g + 1)
                    wait_alone(dve, "dve", e_ready, G * b + g - 2 * G + 1)
                    V.tensor_tensor_reduce(sm[:, s % 2, g, :], ps_s[g % 2][:, 0:NK], mask[:, s % 2, :], 1.0, 3.0e38,
                                           ALU.add, ALU.min, accum_out=neg_max[:, s % 2, g:g + 1]).then_inc(sm_ready, 1)

                if on(b, 0, NB):
                    dve.wait_ge(mask_ready, b + 1)
                    masked(0)
                    masked(1)
                if on(b, 1, NB):
                    copy_probs(0)
                if on(b, 0, NB):
                    masked(2)
                    masked(3)
                if on(b, 1, NB):
                    copy_probs(1)
                if on(b, 0, NB):
                    dve.wait_ge(e_ready, G * b + G)
                    wait(dve, prob_ready, G * b - G)
                    V.reciprocal(recip[:, s % 2, :], row_sum[:, s % 2, :]).then_inc(recip_ready, 1)
                    dve.wait_ge(recip_ready, b + 1)
                    for g in range(G):
                        V.tensor_scalar(prob[:, s % 2, g, :], prob[:, s % 2, g, :], recip[:, s % 2, g:g + 1], None,
                                        ALU.mult).then_inc(prob_ready, 1)
                if turn:
                    dve.wait_ge(wo_done, pair + 1)
                    dve.wait_ge(ld_pair[pair_s], PAIR_DMAS * 16 * j)
                    V.tensor_tensor(x3[:, pair_s, :], ps_x[:, :], x2_in[:, pair_s, :], ALU.add).then_inc(x3_ready, 1)
                if turn:
                    dve.wait_ge(l3_done, pair + 1)
                    dve.wait_ge(x3_ready, pair + 1)
                    wait(dve, st_out[pair_s], 16 * (j - 1))
                    V.scalar_tensor_tensor(x4[:, pair_s, :], ps_x[:, :], sbias[:, pair_s, 0:1], x3[:, pair_s, :],
                                           ALU.add, ALU.add).then_inc(x4_ready, 1)
                if on(b, 1, NB):
                    copy_outputs()
                if on(b, -1, NB):
                    make_mask(b + 1, s + 1)

            loop(dve, phase_two, 4, 8, NB + 3, NB - 4)


def kernel(x, itok_B_0_15, itok_B_0_6, itok_Bx257_0_4111, itok_B_37_3939, itok_B_0_7, fside_8xS_0, L0_cond_W, L0_cond_b,
           L1_cond_W, L1_cond_A, L1_cond_Bm, L1_cond_scalings, L2_cond_Wq, L2_cond_Wk, L2_cond_Wv, L2_cond_Wo,
           L2_cond_q_norm_scale, L2_cond_k_norm_scale, L2_cond_k_blocks, L2_cond_v_blocks, L3_cond_weights):
    import numpy as np
    import concourse.bacc as bacc
    from concourse.bass_utils import run_bass_kernel_spmd

    A = np.ascontiguousarray
    x = np.asarray(x)
    ids = np.stack([np.asarray(itok_B_0_15), np.asarray(itok_B_0_7), np.asarray(itok_B_37_3939)])[None]
    table = np.asarray(itok_Bx257_0_4111)
    padded = np.concatenate([table, np.repeat(table[:, -1:], NWIN + WSLOT - 1 - NSLOT, axis=1)], axis=1)
    windows = np.lib.stride_tricks.sliding_window_view(padded, WSLOT, axis=1)
    wq = np.asarray(L2_cond_Wq).reshape(GP, 2, 2, HD, DC, P).transpose(5, 4, 0, 2, 1, 3)
    wo = np.asarray(L2_cond_Wo).reshape(D, GP, 2, 2, HD).transpose(2, 4, 1, 3, 0)
    kvrows = np.concatenate([np.asarray(t).transpose(0, 2, 1, 3).reshape(NBLK * BLK, G * HD)
                             for t in (L2_cond_k_blocks, L2_cond_v_blocks)], axis=1)
    arrays = {
        "x": A(x.reshape(NP, P, D)),
        "xt": A(x.reshape(NP, P, P, DC).transpose(0, 2, 3, 1)),
        "ids": A(ids),
        "kvl": A(np.asarray(itok_B_37_3939)),
        "adapter": A(np.asarray(itok_B_0_6)),
        "windows": A(windows.reshape(NB * NWIN, WSLOT)),
        "scal": A(np.repeat(np.asarray(L1_cond_scalings), RANK)[:, None]),
        "qn": A(np.asarray(L2_cond_q_norm_scale)),
        "kn": A(np.asarray(L2_cond_k_norm_scale)),
        "w0": A(np.asarray(L0_cond_W).reshape(NE, P, DC * D)),
        "b0": A(np.asarray(L0_cond_b)),
        "w1": A(np.asarray(L1_cond_W).reshape(D, DC, P).transpose(2, 1, 0)),
        "la": A(np.asarray(L1_cond_A).reshape(P, DC, P).transpose(2, 1, 0)),
        "lb": A(np.asarray(L1_cond_Bm).transpose(0, 2, 1).reshape(P, D)),
        "wq": A(wq.reshape(P, DC, D)),
        "wk": A(np.asarray(L2_cond_Wk).reshape(G * HD, DC, P).transpose(2, 1, 0)),
        "wv": A(np.asarray(L2_cond_Wv).reshape(G * HD, DC, P).transpose(2, 1, 0)),
        "wo": A(wo.reshape(P, DC, D)),
        "kvrows": A(kvrows),
        "w3": A(np.asarray(L3_cond_weights)),
        "b3": A(np.asarray(fside_8xS_0)[:, :, None]),
    }
    row = np.arange(P)
    b, half = row % NB, row // NB
    i, t = np.arange(NK)[None, :], (row % T)[:, None]
    fcols = np.zeros((P, 12), np.float32)
    fcols[:, 0] = T * b + 1
    fcols[:, 1] = row // RANK
    fcols[:, 2] = b * NWIN
    for m in range(3):
        fcols[:, 3 + m] = RUNS * b + 2 * m + half
    inv = np.float32(1.0) / np.float32(10000.0) ** (np.arange(HD // 2, dtype=np.float32) / np.float32(HD // 2))
    angle = np.arange(NSLOT * BLK, dtype=np.float32)[:, None] * inv.astype(np.float32)
    cos, sin = np.cos(angle).astype(np.float32), np.sin(angle).astype(np.float32)
    arrays.update({
        "fcols": fcols,
        "mrow": A(np.broadcast_to(np.arange(RUNS * BLK, dtype=np.float32), (P, RUNS * BLK))),
        "runrow": A(np.broadcast_to(np.arange(NRUN, dtype=np.float32), (P, NRUN))),
        "ident": np.eye(P, dtype=np.float32),
        "band": np.where((i > t) & (i <= WIN + t), 0.0, BIG).astype(np.float32),
        "negiota": A(np.broadcast_to(-BIG * i, (P, NK)).astype(np.float32)),
        "rope": A(np.concatenate([cos, cos, sin, sin], axis=1)),
    })
    nc = bacc.Bacc("TRN2", target_bir_lowering=False, num_devices=1)
    aps = {n: nc.dram_tensor("in_" + n, v.shape, mybir.dt.from_np(v.dtype), kind="ExternalInput").ap() for n, v in arrays.items()}
    aps["out"] = nc.dram_tensor("out", (NP, P, D), F32, kind="ExternalOutput").ap()
    build(nc, aps)
    r = run_bass_kernel_spmd(nc, [{"in_" + n: v for n, v in arrays.items()}], core_ids=[0])
    return r.results[0]["out"].reshape(NB, T, D)
```
